# Optimizing a Trainium2 kernel written in Bass

```python
import numpy as np
import jax
import jax.numpy as jnp

def _softmax(x, axis=-1):
    return jax.nn.softmax(x, axis=axis)

def _gelu(x):
    return jax.nn.gelu(x, approximate=True)

def _silu(x):
    return jax.nn.silu(x)

def _sigmoid(x):
    return jax.nn.sigmoid(x)

def _layernorm(x, axis=-1, eps=1e-05):
    m = jnp.mean(x, axis=axis, keepdims=True)
    v = jnp.var(x, axis=axis, keepdims=True)
    return (x - m) / jnp.sqrt(v + eps)

def _scatter_add(tgt, idx, src, axis=0):
    return tgt.at[idx].add(src)

def _segment_sum(src, seg, n):
    return jax.ops.segment_sum(src, seg, n)
kernel_name = 'mk_decoder_postln_d1_seqx_r8_0cf0f8'

def setup_inputs(seed: int=0):
    np.random.seed(seed)
    _w = jnp.asarray

    def _rec_inputs():
        import jax
        import jax.numpy as jnp
        _rk = jax.random.key(seed)
        x = -0.000125 + 0.9999 * jax.random.normal(jax.random.fold_in(_rk, 1), (4, 256, 256), jnp.float32)
        _lenS = 256 - jax.random.randint(jax.random.fold_in(_rk, 7), (4,), 0, max(1, 256 // 4) + 1, jnp.int32)
        _lenS2 = 256 - jax.random.randint(jax.random.fold_in(_rk, 8), (4,), 0, max(1, 256 // 4) + 1, jnp.int32)
        _ctx_2048P = jax.random.normal(jax.random.fold_in(_rk, 11), (4, 16, 256), jnp.float32)
        _ctx_2048c = jax.random.dirichlet(jax.random.fold_in(_rk, 511), 0.3 * jnp.ones((16,), jnp.float32), (4, 256))
        _ctx_2048t = jnp.einsum('bsk,bkd->bsd', _ctx_2048c, _ctx_2048P)
        _ctx_2048t = _ctx_2048t * jax.lax.rsqrt(jnp.mean(jnp.square(_ctx_2048t)) + 1e-12) * 0.953939
        ctx_2048 = -0.00010331 + 0.999899 * (_ctx_2048t + 0.3 * jax.random.normal(jax.random.fold_in(_rk, 611), (4, 256, 256), jnp.float32))
        _validS = jnp.arange(256)[None, :] < _lenS[:, None]
        _validS2 = jnp.arange(256)[None, :] < _lenS2[:, None]
        _causal = jnp.tril(jnp.ones((256, 256), dtype=bool))
        mask_Bx1xS2_ff0 = jnp.where(jnp.ones((4, 1, 256), dtype=bool), 0.0, -1000000000.0).astype(jnp.float32)
        return (x, ctx_2048, mask_Bx1xS2_ff0)
    x, ctx_2048, mask_Bx1xS2_ff0 = _rec_inputs()

    def _L0_attn_setup():
        import jax, jax.numpy as jnp
        import numpy as np
        D_MODEL = 256
        N_HEADS = 16
        SEQ_LEN = 256
        BATCH = 2
        BIAS_MAX = 8.0

        def alibi_bias(n_heads, seq_len, dtype):
            pos = jnp.arange(1 - seq_len, 1, dtype=dtype)
            m = jnp.arange(1, n_heads + 1, dtype=dtype) * (BIAS_MAX / n_heads)
            slopes = 1.0 / 2.0 ** m
            return pos[None, :] * slopes[:, None]
        key = jax.random.key(seed)
        k1, k2, k3 = jax.random.split(key, 3)
        s = 1.0 / np.sqrt(D_MODEL)
        x = jax.random.normal(k1, (BATCH, SEQ_LEN, D_MODEL), dtype=jnp.float32)
        Wqkv = jax.random.normal(k2, (3 * D_MODEL, D_MODEL), dtype=jnp.float32) * s
        b_qkv = jnp.zeros((3 * D_MODEL,), dtype=jnp.float32)
        Wout = jax.random.normal(k3, (D_MODEL, D_MODEL), dtype=jnp.float32) * s
        b_out = jnp.zeros((D_MODEL,), dtype=jnp.float32)
        return {'x': x, 'Wqkv': Wqkv, 'b_qkv': b_qkv, 'Wout': Wout, 'b_out': b_out}
    _L0_attn_all = _L0_attn_setup()
    _L0_attn_in = {k: v for k, v in _L0_attn_all.items() if k in ('Wqkv', 'b_qkv', 'Wout', 'b_out')}
    del _L0_attn_all

    def _L0_xattn_setup():
        import jax, jax.numpy as jnp
        import numpy as np
        FP8_E4M3_MAX = 448.0
        EPS = 1e-12

        def _fp8_quant_dequant(x):
            amax = jnp.max(jnp.abs(x))
            scale = FP8_E4M3_MAX / jnp.maximum(amax, EPS)
            q = jnp.clip(x * scale, -FP8_E4M3_MAX, FP8_E4M3_MAX).astype(jnp.float8_e4m3fn)
            return q.astype(jnp.float32) / scale
        key = jax.random.key(seed)
        k1, k2 = jax.random.split(key)
        B, M, K, N = (32, 64, 256, 256)
        inp = jax.random.normal(k1, (B, M, K), dtype=jnp.float32)
        weight = jax.random.normal(k2, (B, K, N), dtype=jnp.float32)
        bias = jnp.zeros((B, 1, N), dtype=jnp.float32)
        return {'input': inp, 'weight': weight, 'bias': bias}
    _L0_xattn_all = _L0_xattn_setup()
    _L0_xattn_in = {k: v for k, v in _L0_xattn_all.items() if k in ()}
    del _L0_xattn_all

    def _L0_ffn_setup():
        import jax, jax.numpy as jnp
        import numpy as np
        B, S, D, H = (8, 512, 256, 640)

        def ternarize_weight(w):
            abs_mean = jnp.maximum(jnp.mean(jnp.abs(w)), 1e-05)
            thr = 0.7 * abs_mean
            one = jnp.ones((), dtype=w.dtype)
            q = jnp.where(w > thr, one, jnp.where(w < -thr, -one, jnp.zeros((), dtype=w.dtype)))
            return w + jax.lax.stop_gradient(q * abs_mean - w)
        key = jax.random.key(seed)
        k1, k2, k3 = jax.random.split(key, 3)
        x = jax.random.normal(k1, (B, S, D), dtype=jnp.float32)
        w_fc = jax.random.normal(k2, (H, D), dtype=jnp.float32) / np.sqrt(D).astype(np.float32)
        w_proj = jax.random.normal(k3, (D, H), dtype=jnp.float32) / np.sqrt(H).astype(np.float32)
        return {'x': x, 'w_fc': w_fc, 'w_proj': w_proj}
    _L0_ffn_all = _L0_ffn_setup()
    _L0_ffn_in = {k: v for k, v in _L0_ffn_all.items() if k in ('w_fc', 'w_proj')}
    del _L0_ffn_all
    return {'x': x, 'ctx_2048': ctx_2048, 'mask_Bx1xS2_ff0': mask_Bx1xS2_ff0, 'L0_attn_Wqkv': _L0_attn_in['Wqkv'], 'L0_attn_b_qkv': _L0_attn_in['b_qkv'], 'L0_attn_Wout': _L0_attn_in['Wout'], 'L0_attn_b_out': _L0_attn_in['b_out'], 'L0_ffn_w_fc': _L0_ffn_in['w_fc'], 'L0_ffn_w_proj': _L0_ffn_in['w_proj']}

def reference(x, ctx_2048, mask_Bx1xS2_ff0, L0_attn_Wqkv, L0_attn_b_qkv, L0_attn_Wout, L0_attn_b_out, L0_ffn_w_fc, L0_ffn_w_proj):
    import jax
    import jax.numpy as jnp

    def _L0_attn_ref(x, Wqkv, b_qkv, Wout, b_out):
        import jax, jax.numpy as jnp
        import numpy as np
        D_MODEL = 256
        N_HEADS = 16
        SEQ_LEN = 256
        BATCH = 2
        BIAS_MAX = 8.0

        def alibi_bias(n_heads, seq_len, dtype):
            pos = jnp.arange(1 - seq_len, 1, dtype=dtype)
            m = jnp.arange(1, n_heads + 1, dtype=dtype) * (BIAS_MAX / n_heads)
            slopes = 1.0 / 2.0 ** m
            return pos[None, :] * slopes[:, None]
        B, S, D = x.shape
        H = N_HEADS
        hd = D // H
        scale = 1.0 / jnp.sqrt(jnp.asarray(hd, dtype=x.dtype))
        qkv = x @ Wqkv.T + b_qkv
        q, k, v = jnp.split(qkv, 3, axis=-1)
        q = q.reshape(B, S, H, hd)
        k = k.reshape(B, S, H, hd)
        v = v.reshape(B, S, H, hd)
        scores = jnp.einsum('bqhd,bkhd->bhqk', q, k) * scale
        bias = alibi_bias(H, S, x.dtype)
        scores = scores + bias[None, :, None, :]
        causal = jnp.tril(jnp.ones((S, S), dtype=bool))
        scores = jnp.where(causal[None, None, :, :], scores, jnp.asarray(-1000000000.0, dtype=x.dtype))
        p = jax.nn.softmax(scores, axis=-1)
        ctx = jnp.einsum('bhqk,bkhd->bqhd', p, v).reshape(B, S, D)
        return ctx @ Wout.T + b_out

    def _L0_xattn_ref(input, weight, bias):
        import jax, jax.numpy as jnp
        import numpy as np
        FP8_E4M3_MAX = 448.0
        EPS = 1e-12

        def _fp8_quant_dequant(x):
            amax = jnp.max(jnp.abs(x))
            scale = FP8_E4M3_MAX / jnp.maximum(amax, EPS)
            q = jnp.clip(x * scale, -FP8_E4M3_MAX, FP8_E4M3_MAX).astype(jnp.float8_e4m3fn)
            return q.astype(jnp.float32) / scale
        x_dq = _fp8_quant_dequant(input)
        w_dq = _fp8_quant_dequant(weight)
        out = jnp.einsum('bmk,bkn->bmn', x_dq, w_dq)
        out = out + bias
        return out

    def _L0_ffn_ref(x, w_fc, w_proj):
        import jax, jax.numpy as jnp
        import numpy as np
        B, S, D, H = (8, 512, 256, 640)

        def ternarize_weight(w):
            abs_mean = jnp.maximum(jnp.mean(jnp.abs(w)), 1e-05)
            thr = 0.7 * abs_mean
            one = jnp.ones((), dtype=w.dtype)
            q = jnp.where(w > thr, one, jnp.where(w < -thr, -one, jnp.zeros((), dtype=w.dtype)))
            return w + jax.lax.stop_gradient(q * abs_mean - w)
        h = jnp.einsum('bsd,hd->bsh', x, ternarize_weight(w_fc))
        h = jnp.square(jax.nn.relu(h))
        return jnp.einsum('bsh,dh->bsd', h, ternarize_weight(w_proj))
    x = _layernorm(x + _L0_attn_ref(x, L0_attn_Wqkv, L0_attn_b_qkv, L0_attn_Wout, L0_attn_b_out), axis=-1)
    x = _layernorm(x + _L0_xattn_ref(x, ctx_2048, mask_Bx1xS2_ff0), axis=-1)
    x = _layernorm(x + _L0_ffn_ref(x, L0_ffn_w_fc, L0_ffn_w_proj), axis=-1)
    return x

_drawn_inputs = setup_inputs


def setup_inputs(seed=0):
    import zlib

    import numpy as np

    out = dict(_drawn_inputs(seed))
    spreads = {'L0_attn_b_qkv': (0.0, 0.1), 'L0_attn_b_out': (0.0, 0.1)}
    factors = {}
    for name, (base, spread) in spreads.items():
        noise = np.random.default_rng([zlib.crc32(name.encode()), seed]).standard_normal(out[name].shape)
        drawn = base * np.exp(spread * noise) if base else spread * noise
        out[name] = jnp.asarray(drawn.astype(out[name].dtype))
    for name, factor in factors.items():
        out[name] = (out[name] * factor).astype(out[name].dtype)
    return out
```

```python
from contextlib import ExitStack

import numpy as np

import concourse.bass as bass
from concourse import mybir

F32 = mybir.dt.float32
BF16 = mybir.dt.bfloat16
FP16 = mybir.dt.float16
I32 = mybir.dt.int32
ALU = mybir.AluOpType
ACT = mybir.ActivationFunctionType
AX = mybir.AxisListType

P = 128
B, S, D, H = 4, 256, 256, 16
HD = D // H
T = B * S
TB = T // P
DC = D // P
F = 640
FC = F // P
HALF = T // 2
HC = P // HD
PAIRS = H // 2
GROUPS = H // 4

PRODUCTS = [(0, 0), (0, 1), (1, 0), (1, 1), (0, 2), (2, 0)]
ROW_BIAS = HD * len(PRODUCTS)
ROW_MAX = ROW_BIAS + 3
ROWS = ROW_MAX + 3

TRI = P + 2 * P
MASKED = -1.0e9
LN_EPS = 1e-5
FP8_MAX = 448.0
FP8_EPS = 1e-12
EXPONENT = 0x7F800000
FP8_SMALLEST = 2.0 ** -6
H_SCALE = 0.25

BANK_ST, BANK_SM, BANK_O, BANK_Y = 0, 4, 6, 7


def decoder_kernel(nc, x_nat, x_tr, ctx_in, mask_in, w_qk, b_qk, w_v, b_v, w_out, b_out, w_fc, w_proj,
                   alibi, out):
    es = ExitStack()
    with es:
        def sb(name, shape, dt=F32):
            return es.enter_context(nc.sbuf_tensor(name, shape, dt))

        def sem(name):
            return es.enter_context(nc.semaphore(name))

        xT = sb("xT", [P, DC, T])
        x_res = sb("x_res", [P, TB, D])
        wqk = sb("wqk", [P, DC, 4, P])
        bqk = sb("bqk", [P, 4])
        wv = sb("wv", [P, DC, D])
        bv = sb("bv", [P, D])
        bo = sb("bo", [P, D])
        wo = sb("wo", [P, DC, D])
        wfc = sb("wfc", [P, DC, F])
        wpj = sb("wpj", [P, FC, D])
        wfc_t = sb("wfc_t", [P, DC, F], FP16)
        wpj_t = sb("wpj_t", [P, FC, D], FP16)
        kv_ctx = sb("kv_ctx", [P, TB, D])
        kv_q = sb("kv_q", [P, TB, D], BF16)
        maskb = sb("maskb", [P, B, D])
        alibi_f = sb("alibi_f", [H, S])
        alibi_r = sb("alibi_r", [H, 2, S])
        alibi_p = sb("alibi_p", [H, 3, S], BF16)
        ones_b = sb("ones_b", [3, T], BF16)
        ident = sb("ident", [P, P], BF16)
        ident_f = sb("ident_f", [P, P])
        mask_qk = sb("mask_qk", [P, 2, P], BF16)
        mask_kq = sb("mask_kq", [P, 2, P], BF16)
        qk_t = sb("qk_t", [P, 2, HALF])
        qk_r = sb("qk_r", [P, 2, HALF])
        parts = sb("parts", [P, 3, 2, B, DC * S], BF16)
        stack_q = sb("stack_q", [P, B * H * S], BF16)
        stack_k = sb("stack_k", [P, B * H * S], BF16)
        v_nat = sb("v_nat", [P, TB, D])
        v_b = sb("v_b", [P, 2, H, 2 * HD])
        negm = sb("negm", [P, 2, H])
        negm_r = sb("negm_r", [P, 2, 2, H])
        negm_p = sb("negm_p", [P, 2, P // H, H], BF16)
        negm_T = sb("negm_T", [3 * H, S], BF16)
        pT = sb("pT", [P, 4, 2, TRI])
        o_raw = sb("o_raw", [P, GROUPS, S])
        rden = sb("rden", [P, 2, H])
        o_nrm = sb("o_nrm", [P, 2, D])
        oT = sb("oT", [P, DC, S])
        r1 = x_res
        stats = sb("stats", [P, TB, 6])
        mv = sb("mv", [P, TB, 2])
        ve = sb("ve", [P, TB])
        rstd = sb("rstd", [P, TB])
        expo = sb("expo", [P, TB])
        sc = sb("sc", [P, 32])
        qy = sb("qy", [P, 2, 2 * D])
        qw = sb("qw", [P, 2, 2 * D])
        qe = sb("qe", [P, 2, 2 * D])
        qt = qw

        def over(buffer, at, shape, dt):
            n = int(np.prod(shape[1:])) * (2 if dt == F32 else 1)
            letters = "abc"[:len(shape) - 1]
            sizes = dict(zip(letters[1:], shape[2:]))
            flat = buffer[:] if len(buffer.shape) == 2 else buffer[:].rearrange("p a b c d -> p (a b c d)")
            return flat[:, at:at + n].bitcast(dt).rearrange(
                f"p ({' '.join(letters)}) -> p {' '.join(letters)}", **sizes)

        h_hi = over(stack_k, 0, [P, FC, T], FP16)
        h_lo = over(stack_k, FC * T, [P, FC, T], FP16)
        x_qT = over(stack_k, 2 * FC * T, [P, DC, T], BF16)
        x2_hi = over(stack_k, (2 * FC + DC) * T, [P, DC, T], FP16)
        x2_lo = over(stack_k, (2 * FC + 2 * DC) * T, [P, DC, T], FP16)
        x2 = over(parts, 0, [P, TB, D], F32)
        x1m = over(parts, 2 * TB * D, [P, TB, D], F32)
        y_out = over(parts, 4 * TB * D, [P, TB, D], F32)
        x1 = over(stack_q, 0, [P, TB, D], F32)
        x_q = over(stack_q, 2 * TB * D, [P, TB, D], BF16)
        hu, hs = qk_t, qk_r
        w_low = qk_t[:].rearrange("p a n -> p (a n)").bitcast(FP16)[:, 0:FC * D]
        ps = es.enter_context(nc.psum_tensor("ps", [P, 8, 512], F32))

        ld = {n: sem("ld_" + n) for n in (
            "xT0", "xT1", "wqk", "bqk", "x", "wv", "bv", "bo", "wo", "wfc", "wpj", "ctx", "mask", "alibi")}
        consts = sem("consts")
        pool_step = sem("pool_step")
        xres_done = sem("xres_done")
        bq_done = sem("bq_done")
        qk_mm, qk_f32, qk_p0, qk_r1, qk_p1, qk_p2 = (sem(n) for n in (
            "qk_mm", "qk_f32", "qk_p0", "qk_r1", "qk_p1", "qk_p2"))
        stacked = [sem(f"stacked_{b}") for b in range(B)]
        stack_const = sem("stack_const")
        alibi_done = sem("alibi_done")
        v_mm, v_done, vb_done = sem("v_mm"), sem("v_done"), sem("vb_done")
        smax_mm, smax_red, mparts, mT_mm, mT_done, mrows = (sem(n) for n in (
            "smax_mm", "smax_red", "mparts", "mT_mm", "mT_done", "mrows"))
        st_mm, exp_done, pv_mm, o_copied = sem("st_mm"), sem("exp_done"), sem("pv_mm"), sem("o_copied")
        ot_mm, rden_done, o_done, oT_mm, oT_done, y_mm, r1_done = (sem(n) for n in (
            "ot_mm", "rden_done", "o_done", "oT_mm", "oT_done", "y_mm", "r1_done"))
        stat_done, aggr_done = sem("stat_done"), sem("aggr_done")
        ve_done, rstd_done = sem("ve_done"), sem("rstd_done")
        x1_done, x1m_done = sem("x1_done"), sem("x1m_done")
        dve_step = sem("dve_step")
        ctx_max, ctx_all, x_max, x_all, xs_done = (sem(n) for n in (
            "ctx_max", "ctx_all", "x_max", "x_all", "xs_done"))
        wsum, wall = sem("wsum"), sem("wall")
        kvq_done, tern_done = sem("kvq_done"), sem("tern_done")
        xq_done, xqT_mm, xqT_done, xa_mm, r2_done = (sem(n) for n in (
            "xq_done", "xqT_mm", "xqT_done", "xa_mm", "r2_done"))
        x2_done, x2T_mm, x2hi_done, x2lo_done = (sem(n) for n in ("x2_done", "x2T_mm", "x2hi_done", "x2lo_done"))
        f1_mm, hu_done, hs_done, hhi_done, hlo_done, f2_mm, r3_done, y_done = (sem(n) for n in (
            "f1_mm", "hu_done", "hs_done", "hhi_done", "hlo_done", "f2_mm", "r3_done", "y_done"))
        stored = sem("stored")

        def wait(eng, s, value):
            if isinstance(value, int) and value <= 0:
                return
            eng.wait_ge(s, value)

        def cols(b, i, first, count):
            at = (b * H + i) * S + first
            return slice(at, at + count) if isinstance(b, int) else bass.ds(at, count)

        def blocks(b):
            return slice(2 * b, 2 * b + 2) if isinstance(b, int) else bass.ds(2 * b, 2)

        def block(b, i):
            return slice(2 * b + i, 2 * b + i + 1) if isinstance(b, int) else bass.ds(2 * b + i, 1)

        def diag(bank):
            return ps[:, bank, :].rearrange("p (a c) -> p a c", c=2 * P)[:, :, 0:P]

        units = [(half, j) for half in range(2) for j in range(4)]

        def unit_part(n, i):
            half, j = units[n]
            return parts[:, i, j // 2, 2 * half:2 * half + 2, (j % 2) * S:(j % 2 + 1) * S]

        def head(i):
            return HC * (i % 2) + i // 2

        blk_ctx = es.enter_context(nc.Block())

        @blk_ctx.sync
        def _(sp):
            xt_v = x_tr.rearrange("(c p) t -> p c t", p=P)
            sp.dma_start(wqk[:], w_qk.rearrange("(c p) n -> p c n", p=P)).then_inc(ld["wqk"], 16)
            sp.dma_start(xT[:, :, 0:HALF], xt_v[:, :, 0:HALF]).then_inc(ld["xT0"], 16)
            sp.dma_start(xT[:, :, HALF:T], xt_v[:, :, HALF:T]).then_inc(ld["xT1"], 16)
            sp.dma_start(wo[:], w_out.rearrange("(c p) n -> p c n", p=P)).then_inc(ld["wo"], 16)
            sp.dma_start(kv_ctx[:], ctx_in.rearrange("b (c p) n -> p (b c) n", p=P)).then_inc(ld["ctx"], 16)

            sp.wait_ge(consts, 1)
            for stack, row in ((stack_q, ROW_BIAS), (stack_k, ROW_MAX)):
                sp.dma_start(stack[row:row + 3, :].rearrange("p (a t) -> p a t", a=B * H // 4),
                             ones_b[:].unsqueeze(1).to_broadcast([3, B * H // 4, T])).then_inc(stack_const, 16)
            sp.wait_ge(alibi_done, 5)
            for part in range(3):
                for b in range(B):
                    sp.dma_start(stack_k[ROW_BIAS + part:ROW_BIAS + part + 1, b * H * S:(b + 1) * H * S],
                                 alibi_p[:, part, :]).then_inc(stack_const, 16)

            for b in range(B):
                for qk, stack in ((0, stack_q), (1, stack_k)):
                    sp.wait_ge(qk_p2, 4 * (b // 2) + 2 * qk + 2)
                    for g, pair in enumerate(PRODUCTS):
                        sp.dma_start(stack[HD * g:HD * (g + 1), b * H * S:(b + 1) * H * S],
                                     parts[:, pair[qk], qk, b, :]).then_inc(stacked[b], 16)

            def max_rows(b):
                sp.wait_ge(mT_done, b + 1)
                for part in range(3):
                    sp.dma_start(stack_q[ROW_MAX + part:ROW_MAX + part + 1, cols(b, 0, 0, H * S)],
                                 negm_T[H * part:H * (part + 1), :]).then_inc(mrows, 16)

            for b in range(B):
                max_rows(b)

            out_v = out.rearrange("b (c p) n -> p (b c) n", p=P)
            for n in range(TB // 2):
                sp.wait_ge(y_done, 2 * n + 2)
                sp.dma_start(out_v[:, 2 * n:2 * n + 2, :], y_out[:, 2 * n:2 * n + 2, :]).then_inc(stored, 16)
            sp.wait_ge(stored, 16 * (TB // 2))

        @blk_ctx.gpsimd
        def _(pool):
            steps = [0]

            def step(ins):
                steps[0] += 1
                ins.then_inc(pool_step, 1)
                pool.wait_ge(pool_step, steps[0])

            nc.gpsimd.memset(ones_b[:], 1.0).then_inc(consts, 1)
            nc.gpsimd.memset(v_b[:], 1.0)
            nc.gpsimd.memset(expo[:], -0.5)
            nc.gpsimd.memset(negm_p[:], 0.0)
            nc.gpsimd.memset(ident_f[:], 0.0)
            nc.gpsimd.memset(mask_qk[:], 0.0)
            step(nc.gpsimd.memset(mask_kq[:], 0.0))
            nc.gpsimd.affine_select(out=ident_f[:], in_=ident_f[:], compare_op=ALU.not_equal, fill=1.0,
                                    base=0, pattern=[[-1, P]], channel_multiplier=1)
            nc.gpsimd.affine_select(out=mask_qk[:], in_=mask_qk[:], compare_op=ALU.is_ge, fill=MASKED,
                                    base=0, pattern=[[0, 2], [-1, P]], channel_multiplier=1)
            step(nc.gpsimd.affine_select(out=mask_kq[:], in_=mask_kq[:], compare_op=ALU.is_ge, fill=MASKED,
                                         base=0, pattern=[[0, 2], [1, P]], channel_multiplier=-1))
            nc.gpsimd.tensor_copy(ident[:], ident_f[:]).then_inc(consts, 1)
            pool.wait_ge(ld["x"], 16)
            pool.wait_ge(ld["bo"], 16)
            nc.gpsimd.tensor_tensor(out=x_res[:], in0=x_res[:],
                                    in1=bo[:].unsqueeze(1).to_broadcast([P, TB, D]),
                                    op=ALU.add).then_inc(xres_done, 1)
            pool.wait_ge(ctx_max, 1)
            nc.gpsimd.partition_all_reduce(sc[:, 1:2], sc[:, 0:1], P, bass.bass_isa.ReduceOp.max)\
                .then_inc(ctx_all, 1)
            pool.wait_ge(wsum, 2)
            nc.gpsimd.partition_all_reduce(sc[:, 4:6], sc[:, 2:4], P, bass.bass_isa.ReduceOp.add)\
                .then_inc(wall, 1)

            def copy_values(b):
                wait(pool, pv_mm, b * GROUPS)
                nc.gpsimd.tensor_copy(v_b[:, :, :, 0:HD],
                                      v_nat[:, blocks(b), :].rearrange("p k (h d) -> p k h d", h=H))\
                    .then_inc(vb_done, 1)

            pool.wait_ge(v_done, 4)
            copy_values(0)
            with pool.Fori(1, B) as b:
                copy_values(b)

            def rstds(n, lo, hi):
                pool.wait_ge(aggr_done, TB * n + hi)
                nc.gpsimd.tensor_scalar(ve[:, lo:hi], mv[:, lo:hi, 1], LN_EPS, None, ALU.add)\
                    .then_inc(ve_done, 1)
                rs[0] += 1
                pool.wait_ge(ve_done, rs[0])
                nc.gpsimd.tensor_tensor(out=rstd[:, lo:hi], in0=ve[:, lo:hi], in1=expo[:, lo:hi],
                                        op=ALU.pow).then_inc(rstd_done, 1)

            rs = [0]
            rstds(0, 0, TB)
            pool.wait_ge(ld["mask"], 16)
            pool.wait_ge(x1_done, TB)
            pool.wait_ge(x_max, 1)
            nc.gpsimd.partition_all_reduce(sc[:, 11:12], sc[:, 10:11], P, bass.bass_isa.ReduceOp.max)\
                .then_inc(x_all, 1)
            nc.gpsimd.tensor_tensor(out=x1m.rearrange("p (b c) n -> p b c n", b=B),
                                    in0=x1.rearrange("p (b c) n -> p b c n", b=B),
                                    in1=maskb[:].unsqueeze(2).to_broadcast([P, B, 2, D]),
                                    op=ALU.add).then_inc(x1m_done, 1)
            for n in range(TB // 2):
                rstds(1, 2 * n, 2 * n + 2)
            for n in range(TB // 2):
                rstds(2, 2 * n, 2 * n + 2)

        @blk_ctx.scalar
        def _(act):
            act.dma_start(bqk[:], b_qk).then_inc(ld["bqk"], 16)
            act.dma_start(wv[:], w_v.rearrange("(c p) n -> p c n", p=P)).then_inc(ld["wv"], 16)
            act.dma_start(bv[:], b_v.partition_broadcast(P)).then_inc(ld["bv"], 16)
            act.dma_start(alibi_f[:], alibi).then_inc(ld["alibi"], 16)
            act.dma_start(x_res[:], x_nat.rearrange("b (c p) n -> p (b c) n", p=P)).then_inc(ld["x"], 16)
            act.dma_start(bo[:], b_out.partition_broadcast(P)).then_inc(ld["bo"], 16)
            act.dma_start(wfc[:], w_fc.rearrange("(c p) n -> p c n", p=P)).then_inc(ld["wfc"], 16)
            act.dma_start(wpj[:], w_proj.rearrange("(c p) n -> p c n", p=P)).then_inc(ld["wpj"], 16)
            act.dma_start(maskb[:], mask_in.rearrange("b a n -> (a b) n").partition_broadcast(P))\
                .then_inc(ld["mask"], 16)

            act.wait_ge(bq_done, 1)
            for n, (half, j) in enumerate(units):
                act.wait_ge(qk_mm, n + 1)
                wait(act, qk_r1, n - 1)
                nc.scalar.activation(qk_t[:, n % 2, :], ps[:, n, :], ACT.Identity, bias=bqk[:, j:j + 1],
                                     scale=HD ** -0.5 if j < 2 else 1.0).then_inc(qk_f32, 1)
                act.wait_ge(qk_f32, n + 1)
                nc.scalar.activation(unit_part(n, 0), qk_t[:, n % 2, :].rearrange("p (b t) -> p b t", b=2),
                                     ACT.Copy).then_inc(qk_p0, 1)

            def exps(b, p):
                act.wait_ge(st_mm, b * PAIRS + p + 1)
                wait(act, pv_mm, b * GROUPS + p // 2 - 1)
                bank = BANK_ST + 2 * (p % 2)
                nc.scalar.activation(pT[:, p % 4, :, :], ps[:, bank:bank + 2, 0:TRI], ACT.Exp)\
                    .then_inc(exp_done, 1)

            def copy_o(b, i):
                act.wait_ge(pv_mm, b * GROUPS + 2 * i + 2)
                wait(act, ot_mm, b * 2)
                nc.scalar.activation(o_raw[:, 2 * i:2 * i + 2, :].rearrange("p g q -> p (g q)"),
                                     ps[:, BANK_O, :], ACT.Copy).then_inc(o_copied, 1)

            def copy_oT(b):
                act.wait_ge(oT_mm, b + 1)
                wait(act, y_mm, b)
                nc.scalar.activation(oT[:].rearrange("p c q -> p (c q)"), ps[:, BANK_Y, :], ACT.Copy)\
                    .then_inc(oT_done, 1)

            def copy_max(b):
                act.wait_ge(mT_mm, b + 1)
                wait(act, mrows, b * 48)
                nc.scalar.activation(negm_T[:], ps[0:3 * H, BANK_Y, 0:P].bitcast(BF16), ACT.Copy)\
                    .then_inc(mT_done, 1)

            def body(b, prev, nxt):
                for p in range(PAIRS):
                    exps(b, p)
                    if p == 0 and prev:
                        copy_o(b - 1, 1)
                    if p == 4 and prev:
                        copy_oT(b - 1)
                    if p == 5:
                        copy_o(b, 0)
                    if p == 7 and nxt:
                        copy_max(b + 1)

            copy_max(0)
            body(0, False, True)
            with act.Fori(1, B - 1) as b:
                body(b, True, True)
            body(B - 1, True, False)
            copy_o(B - 1, 1)
            copy_oT(B - 1)

            for n in range(TB // 2):
                act.wait_ge(x2T_mm, n + 1)
                nc.scalar.activation(x2_hi[:, :, 2 * n * P:2 * (n + 1) * P],
                                     ps[:, n % 2, :].rearrange("p (c t) -> p c t", c=DC), ACT.Copy)\
                    .then_inc(x2hi_done, 1)
            for n in range(2 * FC + 1):
                if n < 2 * FC:
                    act.wait_ge(f1_mm, n + 1)
                    wait(act, hs_done, n - 1)
                    nc.scalar.activation(hu[:, n % 2, :], ps[:, 2 + n % 4, :], ACT.Relu, scale=H_SCALE)\
                        .then_inc(hu_done, 1)
                if n > 0:
                    half, hc = divmod(n - 1, FC)
                    act.wait_ge(hs_done, n)
                    nc.scalar.activation(h_hi[:, hc, half * HALF:(half + 1) * HALF], hs[:, (n - 1) % 2, :],
                                         ACT.Copy).then_inc(hhi_done, 1)

        @blk_ctx.vector
        def _(dve):
            v = nc.vector
            steps = [0]

            def step(ins):
                steps[0] += 1
                ins.then_inc(dve_step, 1)
                dve.wait_ge(dve_step, steps[0])

            dve.wait_ge(ld["bqk"], 16)
            v.tensor_scalar(bqk[:, 0:2], bqk[:, 0:2], HD ** -0.5, None, ALU.mult).then_inc(bq_done, 1)

            dve.wait_ge(ld["alibi"], 16)
            v.tensor_copy(alibi_p[:, 0, :], alibi_f[:]).then_inc(alibi_done, 1)
            dve.wait_ge(alibi_done, 1)
            v.tensor_tensor(out=alibi_r[:, 0, :], in0=alibi_f[:], in1=alibi_p[:, 0, :], op=ALU.subtract)\
                .then_inc(alibi_done, 1)
            dve.wait_ge(alibi_done, 2)
            v.tensor_copy(alibi_p[:, 1, :], alibi_r[:, 0, :]).then_inc(alibi_done, 1)
            dve.wait_ge(alibi_done, 3)
            v.tensor_tensor(out=alibi_r[:, 1, :], in0=alibi_r[:, 0, :], in1=alibi_p[:, 1, :],
                            op=ALU.subtract).then_inc(alibi_done, 1)
            dve.wait_ge(alibi_done, 4)
            v.tensor_copy(alibi_p[:, 2, :], alibi_r[:, 1, :]).then_inc(alibi_done, 1)

            def qk_parts(n):
                t3, r3 = (a[:, n % 2, :].rearrange("p (b t) -> p b t", b=2) for a in (qk_t, qk_r))
                dve.wait_ge(qk_p0, n + 1)
                v.tensor_tensor(out=r3, in0=t3, in1=unit_part(n, 0), op=ALU.subtract).then_inc(qk_r1, 1)
                dve.wait_ge(qk_r1, n + 1)
                v.tensor_copy(unit_part(n, 1), r3).then_inc(qk_p1, 1)
                dve.wait_ge(qk_p1, n + 1)
                v.tensor_tensor(out=unit_part(n, 2), in0=r3, in1=unit_part(n, 1), op=ALU.subtract)\
                    .then_inc(qk_p2, 1)

            for n in range(8):
                qk_parts(n)
            for n in range(TB // 2):
                dve.wait_ge(v_mm, n + 1)
                if n == 0:
                    dve.wait_ge(ld["bv"], 16)
                v.tensor_tensor(out=v_nat[:, 2 * n:2 * n + 2, :],
                                in0=ps[:, n, :].rearrange("p (k n) -> p k n", k=2),
                                in1=bv[:].unsqueeze(1).to_broadcast([P, 2, D]), op=ALU.add)\
                    .then_inc(v_done, 1)

            def fp8_scale(amax, scale, inverse):
                step(v.tensor_scalar(sc[:, 20:21], amax, FP8_EPS, None, ALU.max))
                step(v.reciprocal(sc[:, 21:22], sc[:, 20:21]))
                v.tensor_scalar(inverse, sc[:, 20:21], 1.0 / FP8_MAX, None, ALU.mult)
                return v.tensor_scalar(scale, sc[:, 21:22], FP8_MAX, None, ALU.mult)

            def quantise(src, dst, scale, signal, n):
                i = n % 2
                step(v.tensor_scalar(qy[:, i, :], src, scale, -FP8_MAX, ALU.mult, ALU.max))
                step(v.tensor_scalar(qw[:, i, :].bitcast(I32), qy[:, i, :].bitcast(I32), EXPONENT, None,
                                     ALU.bitwise_and))
                step(v.tensor_scalar(qe[:, i, :], qw[:, i, :], FP8_SMALLEST, 1.5 * 2.0 ** 20, ALU.max, ALU.mult))
                step(v.scalar_tensor_tensor(qt[:, i, :], qy[:, i, :], FP8_MAX, qe[:, i, :], ALU.min, ALU.add))
                v.tensor_tensor(out=dst, in0=qt[:, i, :], in1=qe[:, i, :], op=ALU.subtract).then_inc(signal, 1)

            dve.wait_ge(ld["ctx"], 16)
            v.tensor_reduce(sc[:, 0:1], kv_ctx[:].rearrange("p a n -> p (a n)"), AX.X, ALU.max,
                            apply_absolute_value=True).then_inc(ctx_max, 1)
            dve.wait_ge(ld["wfc"], 16)
            v.tensor_reduce(sc[:, 2:3], wfc[:].rearrange("p a n -> p (a n)"), AX.X, ALU.add,
                            apply_absolute_value=True).then_inc(wsum, 1)
            dve.wait_ge(ld["wpj"], 16)
            v.tensor_reduce(sc[:, 3:4], wpj[:].rearrange("p a n -> p (a n)"), AX.X, ALU.add,
                            apply_absolute_value=True).then_inc(wsum, 1)
            dve.wait_ge(ctx_all, 1)
            step(fp8_scale(sc[:, 1:2], sc[:, 8:9], sc[:, 9:10]))
            dve.wait_ge(wall, 1)
            step(v.tensor_scalar(sc[:, 14:16], sc[:, 4:6], 1.0 / (D * F), 1e-5, ALU.mult, ALU.max))
            v.tensor_scalar(sc[:, 16:18], sc[:, 14:16], 0.7, None, ALU.mult)
            v.tensor_scalar(sc[:, 18:20], sc[:, 14:16], -0.7, None, ALU.mult)
            step(v.tensor_tensor(out=sc[:, 22:23], in0=sc[:, 14:15], in1=sc[:, 14:15], op=ALU.mult))
            step(v.scalar_tensor_tensor(sc[:, 23:24], sc[:, 22:23], H_SCALE ** -2, sc[:, 15:16],
                                        ALU.mult, ALU.mult))
            for i, (w, wt) in enumerate(((wfc, wfc_t), (wpj, wpj_t))):
                w2, wt2 = (a[:].rearrange("p a n -> p (a n)") for a in (w, wt))
                if i:
                    dve.wait_ge(tern_done, i)
                step(v.tensor_scalar(w_low, w2, sc[:, 18 + i:19 + i], None, ALU.is_lt))
                v.scalar_tensor_tensor(wt2, w2, sc[:, 16 + i:17 + i], w_low, ALU.is_gt, ALU.subtract)\
                    .then_inc(tern_done, 1)

            for n in range(TB // 2):
                if n >= 2:
                    dve.wait_ge(kvq_done, n - 1)
                quantise(kv_ctx[:, 2 * n:2 * n + 2, :].rearrange("p a n -> p (a n)"),
                         kv_q[:, 2 * n:2 * n + 2, :].rearrange("p a n -> p (a n)"), sc[:, 8:9], kvq_done, n)

            def row_max(b, p):
                dve.wait_ge(smax_mm, b * PAIRS + p + 1)
                if p == 0:
                    wait(dve, mparts, b * 5)
                hs2 = slice(2 * p, 2 * p + 2)
                v.tensor_reduce(negm[:, 0, hs2], ps[:, BANK_SM:BANK_SM + 2, 0:P], AX.X, ALU.max, negate=True)
                v.tensor_reduce(negm[:, 1, hs2], ps[:, BANK_SM:BANK_SM + 2, P:TRI], AX.X, ALU.max,
                                negate=True).then_inc(smax_red, 1)

            def max_parts(b):
                dve.wait_ge(smax_red, (b + 1) * PAIRS)
                wait(dve, mT_mm, b)
                if isinstance(b, int) and b == 0:
                    dve.wait_ge(consts, 2)
                v.tensor_copy(negm_p[:, :, 0, :], negm[:]).then_inc(mparts, 1)
                dve.wait_ge(mparts, b * 5 + 1)
                v.tensor_tensor(out=negm_r[:, 0, :, :], in0=negm[:], in1=negm_p[:, :, 0, :], op=ALU.subtract)\
                    .then_inc(mparts, 1)
                dve.wait_ge(mparts, b * 5 + 2)
                v.tensor_copy(negm_p[:, :, 1, :], negm_r[:, 0, :, :]).then_inc(mparts, 1)
                dve.wait_ge(mparts, b * 5 + 3)
                v.tensor_tensor(out=negm_r[:, 1, :, :], in0=negm_r[:, 0, :, :], in1=negm_p[:, :, 1, :],
                                op=ALU.subtract).then_inc(mparts, 1)
                dve.wait_ge(mparts, b * 5 + 4)
                v.tensor_copy(negm_p[:, :, 2, :], negm_r[:, 1, :, :]).then_inc(mparts, 1)

            def normalise(b, i):
                dve.wait_ge(ot_mm, 2 * b + i + 1)
                wait(dve, oT_mm, b)
                heads = ps[:, BANK_Y, :].rearrange("p (h d) -> p h d", d=2 * HD)
                v.reciprocal(rden[:, i, :].unsqueeze(2), heads[:, :, HD:HD + 1]).then_inc(rden_done, 1)
                dve.wait_ge(rden_done, 2 * b + i + 1)
                for c in range(DC):
                    last = v.tensor_tensor(out=o_nrm[:, i, c * P:(c + 1) * P].rearrange("p (h d) -> p h d", d=HD),
                                           in0=heads[:, c:H:DC, 0:HD],
                                           in1=rden[:, i, c:H:DC].unsqueeze(2).to_broadcast([P, HC, HD]),
                                           op=ALU.mult)
                last.then_inc(o_done, 1)

            def add_residual(b):
                dve.wait_ge(y_mm, b + 1)
                if isinstance(b, int) and b == 0:
                    dve.wait_ge(xres_done, 1)
                v.tensor_tensor(out=r1[:, blocks(b), :], in0=ps[:, BANK_Y, :].rearrange("p (k n) -> p k n", k=2),
                                in1=x_res[:, blocks(b), :], op=ALU.add).then_inc(r1_done, 1)
                dve.wait_ge(r1_done, b + 1)
                for i in range(2):
                    v.bn_stats(stats[:, block(b, i), :], r1[:, block(b, i), :]).then_inc(stat_done, 1)

            def body(b, prev, nxt):
                if nxt:
                    row_max(b + 1, 0)
                    row_max(b + 1, 1)
                    row_max(b + 1, 2)
                if prev:
                    normalise(b - 1, 0)
                if nxt:
                    row_max(b + 1, 3)
                    row_max(b + 1, 4)
                if prev:
                    normalise(b - 1, 1)
                if nxt:
                    row_max(b + 1, 5)
                    row_max(b + 1, 6)
                if prev:
                    add_residual(b - 1)
                if nxt:
                    row_max(b + 1, 7)
                    max_parts(b + 1)

            for p in range(PAIRS):
                row_max(0, p)
            max_parts(0)
            body(0, False, True)
            with dve.Fori(1, B - 1) as b:
                body(b, True, True)
            body(B - 1, True, False)
            normalise(B - 1, 0)
            normalise(B - 1, 1)
            add_residual(B - 1)

            dve.wait_ge(stat_done, TB)
            for k in range(TB):
                v.bn_aggr(mv[:, k, :], stats[:, k, :]).then_inc(aggr_done, 1)
            dve.wait_ge(rstd_done, 1)
            for k in range(TB):
                ins = v.tensor_scalar(x1[:, k, :], r1[:, k, :], mv[:, k, 0:1], rstd[:, k:k + 1],
                                      ALU.subtract, ALU.mult).then_inc(x1_done, 1)
            dve.wait_ge(x1_done, TB)
            v.tensor_reduce(sc[:, 10:11], x1.rearrange("p a n -> p (a n)"), AX.X, ALU.max,
                            apply_absolute_value=True).then_inc(x_max, 1)
            dve.wait_ge(x_all, 1)
            step(fp8_scale(sc[:, 11:12], sc[:, 12:13], sc[:, 13:14]))
            v.tensor_tensor(out=sc[:, 24:25], in0=sc[:, 13:14], in1=sc[:, 9:10], op=ALU.mult)\
                .then_inc(xs_done, 1)
            for n in range(TB // 2):
                if n >= 2:
                    dve.wait_ge(xq_done, n - 1)
                quantise(x1[:, 2 * n:2 * n + 2, :].rearrange("p a n -> p (a n)"),
                         x_q[:, 2 * n:2 * n + 2, :].rearrange("p a n -> p (a n)"), sc[:, 12:13], xq_done, n)
                dve.wait_ge(xqT_mm, n + 1)
                v.tensor_copy(x_qT[:, :, 2 * n * P:2 * (n + 1) * P],
                              ps[:, n % 2, 0:2 * P].bitcast(BF16).rearrange("p (c t) -> p c t", c=DC))\
                    .then_inc(xqT_done, 1)

            dve.wait_ge(x1m_done, 1)
            dve.wait_ge(xs_done, 1)
            for n in range(TB // 2):
                dve.wait_ge(xa_mm, n + 1)
                v.scalar_tensor_tensor(r1[:, 2 * n:2 * n + 2, :].rearrange("p a n -> p (a n)"),
                                       ps[:, 2 + n, :], sc[:, 24:25],
                                       x1m[:, 2 * n:2 * n + 2, :].rearrange("p a n -> p (a n)"),
                                       ALU.mult, ALU.add).then_inc(r2_done, 1)
                dve.wait_ge(r2_done, n + 1)
                for k in (2 * n, 2 * n + 1):
                    v.bn_stats(stats[:, k, :], r1[:, k, :]).then_inc(stat_done, 1)
                for k in (2 * n, 2 * n + 1):
                    dve.wait_ge(stat_done, TB + k + 1)
                    v.bn_aggr(mv[:, k, :], stats[:, k, :]).then_inc(aggr_done, 1)
            for n in range(TB // 2):
                dve.wait_ge(rstd_done, 2 + n)
                for k in (2 * n, 2 * n + 1):
                    v.tensor_scalar(x2[:, k, :], r1[:, k, :], mv[:, k, 0:1], rstd[:, k:k + 1],
                                    ALU.subtract, ALU.mult).then_inc(x2_done, 1)
            for n in range(TB // 2):
                dve.wait_ge(x2hi_done, n + 1)
                v.tensor_tensor(out=x2_lo[:, :, 2 * n * P:2 * (n + 1) * P],
                                in0=ps[:, n % 2, :].rearrange("p (c t) -> p c t", c=DC),
                                in1=x2_hi[:, :, 2 * n * P:2 * (n + 1) * P], op=ALU.subtract)\
                    .then_inc(x2lo_done, 1)
            for n in range(2 * FC):
                half, hc = divmod(n, FC)
                dve.wait_ge(hu_done, n + 1)
                wait(dve, hhi_done, n - 1)
                v.tensor_tensor(out=hs[:, n % 2, :], in0=hu[:, n % 2, :], in1=hu[:, n % 2, :], op=ALU.mult)\
                    .then_inc(hs_done, 1)
                dve.wait_ge(hhi_done, n + 1)
                v.tensor_tensor(out=h_lo[:, hc, half * HALF:(half + 1) * HALF], in0=hs[:, n % 2, :],
                                in1=h_hi[:, hc, half * HALF:(half + 1) * HALF], op=ALU.subtract)\
                    .then_inc(hlo_done, 1)
            for n in range(TB // 2):
                dve.wait_ge(f2_mm, n + 1)
                v.scalar_tensor_tensor(r1[:, 2 * n:2 * n + 2, :].rearrange("p a n -> p (a n)"),
                                       ps[:, 6 + n % 2, :], sc[:, 23:24],
                                       x2[:, 2 * n:2 * n + 2, :].rearrange("p a n -> p (a n)"),
                                       ALU.mult, ALU.add).then_inc(r3_done, 1)
                dve.wait_ge(r3_done, n + 1)
                for k in (2 * n, 2 * n + 1):
                    v.bn_stats(stats[:, k, :], r1[:, k, :]).then_inc(stat_done, 1)
                for k in (2 * n, 2 * n + 1):
                    dve.wait_ge(stat_done, 2 * TB + k + 1)
                    v.bn_aggr(mv[:, k, :], stats[:, k, :]).then_inc(aggr_done, 1)
                dve.wait_ge(rstd_done, 6 + n)
                for k in (2 * n, 2 * n + 1):
                    v.tensor_scalar(y_out[:, k, :], r1[:, k, :], mv[:, k, 0:1], rstd[:, k:k + 1],
                                    ALU.subtract, ALU.mult).then_inc(y_done, 1)

        @blk_ctx.tensor
        def _(pe):
            mm = nc.tensor.matmul
            pe.wait_ge(ld["wqk"], 16)
            for n, (half, j) in enumerate(units):
                if j == 0:
                    pe.wait_ge(ld[f"xT{half}"], 16)
                for c in range(DC):
                    last = mm(ps[:, n, :], wqk[:, c, j, :], xT[:, c, half * HALF:(half + 1) * HALF],
                              start=(c == 0), stop=(c == DC - 1))
                last.then_inc(qk_mm, 1)
            pe.wait_ge(ld["wv"], 16)
            for n in range(TB // 2):
                pe.wait_ge(qk_f32, n + 1)
                for i in range(2):
                    k = 2 * n + i
                    for c in range(DC):
                        last = mm(ps[:, n, i * D:(i + 1) * D], xT[:, c, k * P:(k + 1) * P], wv[:, c, :],
                                  start=(c == 0), stop=(c == DC - 1))
                last.then_inc(v_mm, 1)

            def score_max(b, p):
                wait(pe, smax_red, b * PAIRS + p)
                for e in range(2):
                    h, bank = 2 * p + e, BANK_SM + e
                    mm(diag(bank), ident[:], mask_qk[:], start=True, stop=False, skip_group_check=True)
                    mm(ps[:, bank, 0:P], stack_q[0:ROW_MAX, cols(b, h, 0, P)], stack_k[0:ROW_MAX, cols(b, h, 0, P)],
                       start=False, stop=False, skip_group_check=True)
                    last = mm(ps[:, bank, P:TRI], stack_q[0:ROW_MAX, cols(b, h, P, P)],
                              stack_k[0:ROW_MAX, cols(b, h, 0, S)], start=False, stop=True, skip_group_check=True)
                last.then_inc(smax_mm, 1)

            def scores(b, p):
                if p == 0:
                    pe.wait_ge(mrows, (b + 1) * 48)
                wait(pe, exp_done, b * PAIRS + p - 1)
                for e in range(2):
                    h, bank = 2 * p + e, BANK_ST + 2 * (p % 2) + e
                    mm(diag(bank), ident[:], mask_kq[:], start=True, stop=False, skip_group_check=True)
                    mm(ps[:, bank, 0:S], stack_k[0:ROWS, cols(b, h, 0, P)], stack_q[0:ROWS, cols(b, h, 0, S)],
                       start=False, stop=False, skip_group_check=True)
                    last = mm(ps[:, bank, S:TRI], stack_k[0:ROWS, cols(b, h, P, P)], stack_q[0:ROWS, cols(b, h, P, P)],
                              start=False, stop=True, skip_group_check=True)
                last.then_inc(st_mm, 1)

            def max_to_rows(b):
                pe.wait_ge(mparts, (b + 1) * 5)
                wait(pe, r1_done, b - 1)
                for i in range(2):
                    last = nc.tensor.transpose(ps[:, BANK_Y, i * P // 2:(i + 1) * P // 2].bitcast(BF16),
                                               negm_p[:, i, :, :].rearrange("p a h -> p (a h)"), ident[:])
                last.then_inc(mT_mm, 1)

            def values(b, g):
                pe.wait_ge(exp_done, b * PAIRS + 2 * g + 2)
                if g == 0:
                    pe.wait_ge(vb_done, b + 1)
                if g % 2 == 0:
                    wait(pe, o_copied, 2 * b + g // 2)
                o = (g % 2) * S
                for k in range(2):
                    for j in range(4):
                        prob = pT[:, (2 * g + j // 2) % 4, j % 2, :]
                        last = mm(ps[32 * j:32 * j + 32, BANK_O, o + k * P:o + S], v_b[:, k, head(4 * g + j), :],
                                  prob[:, 0:S] if k == 0 else prob[:, S:TRI], start=(k == 0), stop=(k == 1),
                                  skip_group_check=True)
                last.then_inc(pv_mm, 1)

            def queries_down(b, i):
                if i == 0:
                    pe.wait_ge(o_copied, 2 * b + 2)
                    pe.wait_ge(mT_done, b + 1)
                    wait(pe, r1_done, b)
                else:
                    pe.wait_ge(o_done, 2 * b + 1)
                for g in range(GROUPS):
                    last = nc.tensor.transpose(ps[:, BANK_Y, g * P:(g + 1) * P],
                                               o_raw[:, g, i * P:(i + 1) * P], ident_f[:])
                last.then_inc(ot_mm, 1)

            def features_down(b):
                pe.wait_ge(o_done, 2 * b + 2)
                for i in range(2):
                    for c in range(DC):
                        last = nc.tensor.transpose(ps[:, BANK_Y, c * S + i * P:c * S + (i + 1) * P],
                                                   o_nrm[:, i, c * P:(c + 1) * P], ident_f[:])
                last.then_inc(oT_mm, 1)

            def project(b):
                pe.wait_ge(oT_done, b + 1)
                for i in range(2):
                    for c in range(DC):
                        last = mm(ps[:, BANK_Y, i * D:(i + 1) * D], oT[:, c, i * P:(i + 1) * P], wo[:, c, :],
                                  start=(c == 0), stop=(c == DC - 1))
                last.then_inc(y_mm, 1)

            def body(b, prev, nxt):
                scores(b, 0)
                if prev:
                    values(b - 1, 3)
                if nxt:
                    score_max(b + 1, 0)
                    score_max(b + 1, 1)
                scores(b, 1)
                if prev:
                    queries_down(b - 1, 0)
                if nxt:
                    score_max(b + 1, 2)
                    score_max(b + 1, 3)
                scores(b, 2)
                if prev:
                    queries_down(b - 1, 1)
                if nxt:
                    score_max(b + 1, 4)
                scores(b, 3)
                values(b, 0)
                if prev:
                    features_down(b - 1)
                if nxt:
                    score_max(b + 1, 5)
                scores(b, 4)
                if prev:
                    project(b - 1)
                if nxt:
                    score_max(b + 1, 6)
                scores(b, 5)
                values(b, 1)
                if nxt:
                    score_max(b + 1, 7)
                scores(b, 6)
                scores(b, 7)
                if nxt:
                    if prev:
                        pe.wait_ge(r1_done, b)
                    max_to_rows(b + 1)
                values(b, 2)

            pe.wait_ge(consts, 2)
            pe.wait_ge(stacked[0], 12 * 16)
            pe.wait_ge(stack_const, 14 * 16)
            pe.wait_ge(qk_f32, 8)
            pe.wait_ge(v_done, 4)
            for p in range(PAIRS):
                score_max(0, p)
            max_to_rows(0)
            pe.wait_ge(stacked[1], 12 * 16)
            pe.wait_ge(ld["wo"], 16)
            body(0, False, True)
            pe.wait_ge(stacked[2], 12 * 16)
            pe.wait_ge(stacked[3], 12 * 16)
            with pe.Fori(1, B - 1) as b:
                body(b, True, True)
            body(B - 1, True, False)
            values(B - 1, 3)
            queries_down(B - 1, 0)
            queries_down(B - 1, 1)
            features_down(B - 1)
            project(B - 1)

            pe.wait_ge(exp_done, B * PAIRS)
            pe.wait_ge(kvq_done, 4)
            pe.wait_ge(r1_done, B)
            for n in range(TB // 2):
                pe.wait_ge(xq_done, n + 1)
                wait(pe, xqT_done, n - 1)
                tr = ps[:, n % 2, 0:2 * P].bitcast(BF16)
                for i in range(2):
                    for c in range(DC):
                        last = nc.tensor.transpose(tr[:, c * S + i * P:c * S + (i + 1) * P],
                                                   x_q[:, 2 * n + i, c * P:(c + 1) * P], ident[:])
                last.then_inc(xqT_mm, 1)
                pe.wait_ge(xqT_done, n + 1)
                for i in range(2):
                    k = 2 * n + i
                    for c in range(DC):
                        last = mm(ps[:, 2 + n, i * D:(i + 1) * D], x_qT[:, c, k * P:(k + 1) * P],
                                  kv_q[:, 2 * n + c, :], start=(c == 0), stop=(c == DC - 1))
                last.then_inc(xa_mm, 1)

            for n in range(TB // 2):
                pe.wait_ge(x2_done, 2 * n + 2)
                wait(pe, x2lo_done, n - 1)
                for i in range(2):
                    for c in range(DC):
                        last = nc.tensor.transpose(ps[:, n % 2, c * S + i * P:c * S + (i + 1) * P],
                                                   x2[:, 2 * n + i, c * P:(c + 1) * P], ident_f[:])
                last.then_inc(x2T_mm, 1)
            pe.wait_ge(tern_done, 2)
            pe.wait_ge(r2_done, 4)
            for n in range(2 * FC):
                half, hc = divmod(n, FC)
                if hc == 0:
                    pe.wait_ge(x2lo_done, 2 * half + 2)
                wait(pe, hu_done, n - 3)
                for c in range(DC):
                    for part in (x2_hi, x2_lo):
                        last = mm(ps[:, 2 + n % 4, :], wfc_t[:, c, hc * P:(hc + 1) * P],
                                  part[:, c, half * HALF:(half + 1) * HALF],
                                  start=(c == 0 and part is x2_hi), stop=(c == DC - 1 and part is x2_lo))
                last.then_inc(f1_mm, 1)
            for n in range(TB // 2):
                pe.wait_ge(hlo_done, FC * (n // 2 + 1))
                wait(pe, r3_done, n - 1)
                for i in range(2):
                    k = 2 * n + i
                    for hc in range(FC):
                        for part in (h_hi, h_lo):
                            last = mm(ps[:, 6 + n % 2, i * D:(i + 1) * D], part[:, hc, k * P:(k + 1) * P],
                                      wpj_t[:, hc, :], start=(hc == 0 and part is h_hi),
                                      stop=(hc == FC - 1 and part is h_lo))
                last.then_inc(f2_mm, 1)


def kernel(x, ctx_2048, mask_Bx1xS2_ff0, L0_attn_Wqkv, L0_attn_b_qkv, L0_attn_Wout, L0_attn_b_out,
           L0_ffn_w_fc, L0_ffn_w_proj):
    import numpy as _np
    import concourse.bacc as _bacc
    from concourse import mybir as _mybir
    from concourse.bass_utils import run_bass_kernel_spmd as _run

    x, ctx, mask, wqkv, bqkv, wout, bout, wfc, wproj = (_np.asarray(a) for a in (
        x, ctx_2048, mask_Bx1xS2_ff0, L0_attn_Wqkv, L0_attn_b_qkv, L0_attn_Wout, L0_attn_b_out,
        L0_ffn_w_fc, L0_ffn_w_proj))
    w_qk = wqkv[:2 * D].reshape(4, HC, HD, D).transpose(3, 0, 2, 1).reshape(D, 4 * P)
    b_qk = bqkv[:2 * D].reshape(4, HC, HD).transpose(2, 1, 0).reshape(P, 4)
    slopes = 1.0 / 2.0 ** (_np.arange(1, H + 1, dtype=_np.float32) * _np.float32(8.0 / H))
    alibi = _np.arange(1 - S, 1, dtype=_np.float32)[None, :] * slopes.astype(_np.float32)[:, None]
    alibi = alibi.reshape(2, HC, S).transpose(1, 0, 2).reshape(H, S)
    arrays = {
        "x_nat": x, "x_tr": x.reshape(T, D).T, "ctx_in": ctx, "mask_in": mask, "w_qk": w_qk, "b_qk": b_qk,
        "w_v": wqkv[2 * D:].T, "b_v": bqkv[2 * D:], "w_out": wout.T, "b_out": bout,
        "w_fc": wfc.T, "w_proj": wproj.T, "alibi": alibi,
    }
    arrays = {n: _np.ascontiguousarray(a) for n, a in arrays.items()}
    nc = _bacc.Bacc("TRN2", target_bir_lowering=False, num_devices=1)
    args = [nc.dram_tensor(n, a.shape, _mybir.dt.from_np(a.dtype), kind="ExternalInput").ap()
            for n, a in arrays.items()]
    y = nc.dram_tensor("y", (B, S, D), F32, kind="ExternalOutput").ap()
    decoder_kernel(nc, *args, y)
    r = _run(nc, [arrays], core_ids=[0])
    return r.results[0]["y"]
```

```python
from contextlib import ExitStack

import numpy as np

import concourse.bass as bass
from concourse import mybir

F32 = mybir.dt.float32
BF16 = mybir.dt.bfloat16
FP16 = mybir.dt.float16
I32 = mybir.dt.int32
ALU = mybir.AluOpType
ACT = mybir.ActivationFunctionType
AX = mybir.AxisListType

P = 128
B, S, D, H = 4, 256, 256, 16
HD = D // H
T = B * S
TB = T // P
DC = D // P
F = 640
FC = F // P
HALF = T // 2
HC = P // HD
PAIRS = H // 2
GROUPS = H // 4

PRODUCTS = [(0, 0), (0, 1), (1, 0), (1, 1), (0, 2), (2, 0)]
ROW_BIAS = HD * len(PRODUCTS)
ROW_MAX = ROW_BIAS + 3
ROWS = ROW_MAX + 3

TRI = P + 2 * P
MASKED = -1.0e9
LN_EPS = 1e-5
FP8_MAX = 448.0
FP8_EPS = 1e-12
EXPONENT = 0x7F800000
FP8_SMALLEST = 2.0 ** -6
H_SCALE = 0.25

BANK_SM, BANK_ST, BANK_O, BANK_Y = 0, 4, 6, 7
MT_BANK = (3, 3)
F1_BANKS = (6, 7, 0, 1)
P_SLOTS = 8


def decoder_kernel(nc, x_nat, x_tr, ctx_in, mask_in, w_qk, b_qk, w_v, b_v, w_out, b_out, w_fc, w_proj,
                   alibi, out):
    es = ExitStack()
    with es:
        def sb(name, shape, dt=F32):
            return es.enter_context(nc.sbuf_tensor(name, shape, dt))

        def sem(name):
            return es.enter_context(nc.semaphore(name))

        xT = sb("xT", [P, DC, T])
        x_res = sb("x_res", [P, TB, D])
        wqk = sb("wqk", [P, DC, 4, P])
        bqk = sb("bqk", [P, 4])
        wv = sb("wv", [P, DC, D])
        bv = sb("bv", [P, D])
        bo = sb("bo", [P, D])
        wo = sb("wo", [P, DC, D])
        wfc = sb("wfc", [P, DC, F])
        wpj = sb("wpj", [P, FC, D])
        wfc_t = sb("wfc_t", [P, DC, F], FP16)
        wpj_t = sb("wpj_t", [P, FC, D], FP16)
        w_low = sb("w_low", [P, FC * D], FP16)
        kv_ctx = sb("kv_ctx", [P, TB, D])
        kv_q = sb("kv_q", [P, TB, D], BF16)
        maskb = sb("maskb", [P, B, D])
        ones_b = sb("ones_b", [3, T], BF16)
        ident = sb("ident", [P, P], BF16)
        ident_f = sb("ident_f", [P, P])
        mask_qk = sb("mask_qk", [P, 2, P], BF16)
        mask_kq = sb("mask_kq", [P, 2, P], BF16)
        qk_t = sb("qk_t", [P, 2, HALF])
        qk_r = sb("qk_r", [P, 2, HALF])
        parts = sb("parts", [P, 3, 2, B, DC * S], BF16)
        stack_q = sb("stack_q", [P, B * H * S], BF16)
        stack_k = sb("stack_k", [P, B * H * S], BF16)
        v_nat = sb("v_nat", [P, TB, D])
        v_ones = sb("v_ones", [P, 2, H, 2 * HD])
        negm3 = sb("negm3", [P, H, 3])
        negm_r = sb("negm_r", [P, 2, 2, HC])
        negm_p = sb("negm_p", [P, 2, 2, P // HC, HC], BF16)
        negm_T = sb("negm_T", [3 * HC, 2, S], BF16)
        pT = sb("pT", [P, P_SLOTS, TRI])
        o_raw = sb("o_raw", [P, GROUPS, S])
        rden = sb("rden", [P, 2, H])
        o_nrm = sb("o_nrm", [P, 2, D])
        oT = sb("oT", [P, DC, S])
        r1 = x_res
        stats = sb("stats", [P, 2, 6])
        mv = sb("mv", [P, 2, 2, 2])
        ve = sb("ve", [P, 2, 2])
        rstd = sb("rstd", [P, 2, 2])
        expo = sb("expo", [P, 2])
        amax = sb("amax", [P, B])
        sc = sb("sc", [P, 32])
        qe = sb("qe", [P, 2, 2 * D])

        def over(buffer, at, shape, dt):
            n = int(np.prod(shape[1:])) * (2 if dt == F32 else 1)
            letters = "abc"[:len(shape) - 1]
            sizes = dict(zip(letters[1:], shape[2:]))
            flat = buffer[:] if len(buffer.shape) == 2 else buffer[:].rearrange("p a b c d -> p (a b c d)")
            return flat[:, at:at + n].bitcast(dt).rearrange(
                f"p ({' '.join(letters)}) -> p {' '.join(letters)}", **sizes)

        h_hi = over(stack_k, 0, [P, FC, T], FP16)
        h_lo = over(stack_k, FC * T, [P, FC, T], FP16)
        x_qT = over(stack_k, 2 * FC * T, [P, DC, T], BF16)
        x2_hi = over(stack_k, (2 * FC + DC) * T, [P, DC, T], FP16)
        x2_lo = over(stack_k, (2 * FC + 2 * DC) * T, [P, DC, T], FP16)
        x2 = over(parts, 0, [P, TB, D], F32)
        x1m = over(parts, 2 * TB * D, [P, TB, D], F32)
        y_out = over(parts, 4 * TB * D, [P, TB, D], F32)
        x1 = over(stack_q, 0, [P, TB, D], F32)
        x_q = over(stack_q, 2 * TB * D, [P, TB, D], BF16)
        hu, hs = qk_t, qk_r
        magic = xT[:].rearrange("p c (a n) -> p (c a) n", n=D)
        xy = kv_ctx
        ps = es.enter_context(nc.psum_tensor("ps", [P, 8, 512], F32))

        ld = {n: sem("ld_" + n) for n in (
            "xT0", "xT1", "wqk", "bqk", "x", "wv", "bv", "bo", "wo", "wfc", "wpj", "ctx", "mask")}
        consts = sem("consts")
        pool_step = sem("pool_step")
        xres_done = sem("xres_done")
        bq_done = sem("bq_done")
        qk_mm, qk_f32, qk_p0, qk_r1, qk_p1, qk_p2 = (sem(n) for n in (
            "qk_mm", "qk_f32", "qk_p0", "qk_r1", "qk_p1", "qk_p2"))
        stacked = [sem(f"stacked_{b}") for b in range(B)]
        stack_const = sem("stack_const")
        v_mm, v_done, vb_done = sem("v_mm"), sem("v_done"), sem("vb_done")
        smax_mm, smax_red, mparts, mT_mm, mT_done, mrows = (sem(n) for n in (
            "smax_mm", "smax_red", "mparts", "mT_mm", "mT_done", "mrows"))
        st_mm, exp_done, pv_mm, o_copied = (sem(n) for n in (
            "st_mm", "exp_done", "pv_mm", "o_copied"))
        ot_mm, rden_done, o_done, oT_mm, oT_done, y_mm, r1_done = (sem(n) for n in (
            "ot_mm", "rden_done", "o_done", "oT_mm", "oT_done", "y_mm", "r1_done"))
        stat_done, aggr_done = sem("stat_done"), sem("aggr_done")
        ve_done, rstd_done = sem("ve_done"), sem("rstd_done")
        x1_done, x1m_done = sem("x1_done"), sem("x1m_done")
        dve_step = sem("dve_step")
        ctx_max, ctx_all, x_max, x_all, xs_done = (sem(n) for n in (
            "ctx_max", "ctx_all", "x_max", "x_all", "xs_done"))
        wsum, wall = sem("wsum"), sem("wall")
        kvq_done, tern_done, ctx_scaled, kv_scaled, kv_clipped, kv_magic = (sem(n) for n in (
            "kvq_done", "tern_done", "ctx_scaled", "kv_scaled", "kv_clipped", "kv_magic"))
        b_max, x_scaled = sem("b_max"), sem("x_scaled")
        xq_done, xqT_mm, xqT_done, xa_mm, r2_done = (sem(n) for n in (
            "xq_done", "xqT_mm", "xqT_done", "xa_mm", "r2_done"))
        x2_done, x2T_mm, x2hi_done, x2lo_done = (sem(n) for n in ("x2_done", "x2T_mm", "x2hi_done", "x2lo_done"))
        f1_mm, hu_done, hs_done, hhi_done, hlo_done, f2_mm, r3_done, y_done = (sem(n) for n in (
            "f1_mm", "hu_done", "hs_done", "hhi_done", "hlo_done", "f2_mm", "r3_done", "y_done"))
        stored = sem("stored")

        def wait(eng, s, value):
            if isinstance(value, int) and value <= 0:
                return
            eng.wait_ge(s, value)

        def wait_apart(eng, s, value):
            if isinstance(value, int):
                eng.wait_ge(s, value)
            else:
                value = eng.snap(eng.to_reg(value))
                eng.wait_ge(s, 1)
                eng.wait_ge(s, value)

        def cols(b, i, first, count):
            at = (b * H + i) * S + first
            return slice(at, at + count) if isinstance(b, int) else bass.ds(at, count)

        def blocks(b):
            return slice(2 * b, 2 * b + 2) if isinstance(b, int) else bass.ds(2 * b, 2)

        def block(b, i):
            return slice(2 * b + i, 2 * b + i + 1) if isinstance(b, int) else bass.ds(2 * b + i, 1)

        def diag(bank):
            return ps[:, bank, :].rearrange("p (a c) -> p a c", c=2 * P)[:, :, 0:P]

        units = [(half, j) for half in range(2) for j in range(4)]

        def unit_part(n, i):
            half, j = units[n]
            return parts[:, i, j // 2, 2 * half:2 * half + 2, (j % 2) * S:(j % 2 + 1) * S]

        def head(i):
            return HC * (i % 2) + i // 2

        blk_ctx = es.enter_context(nc.Block())

        @blk_ctx.sync
        def _(sp):
            xt_v = x_tr.rearrange("(c p) t -> p c t", p=P)
            sp.dma_start(wqk[:], w_qk.rearrange("(c p) n -> p c n", p=P)).then_inc(ld["wqk"], 16)
            sp.dma_start(xT[:, :, 0:HALF], xt_v[:, :, 0:HALF]).then_inc(ld["xT0"], 16)
            sp.dma_start(xT[:, :, HALF:T], xt_v[:, :, HALF:T]).then_inc(ld["xT1"], 16)
            sp.dma_start(wo[:], w_out.rearrange("(c p) n -> p c n", p=P)).then_inc(ld["wo"], 16)
            sp.dma_start(x_res[:], x_nat.rearrange("b (c p) n -> p (b c) n", p=P)).then_inc(ld["x"], 16)
            sp.dma_start(bo[:], b_out.partition_broadcast(P)).then_inc(ld["bo"], 16)

            for b in range(B):
                for qk, stack in ((0, stack_q), (1, stack_k)):
                    sp.wait_ge(qk_p2, 4 * (b // 2) + 2 * qk + 2)
                    for g, pair in enumerate(PRODUCTS):
                        sp.dma_start(stack[HD * g:HD * (g + 1), cols(b, 0, 0, H * S)],
                                     parts[:, pair[qk], qk, b, :]).then_inc(stacked[b], 16)

            sp.dma_start(maskb[:], mask_in.rearrange("b a n -> (a b) n").partition_broadcast(P))\
                .then_inc(ld["mask"], 16)

            out_v = out.rearrange("b (c p) n -> p (b c) n", p=P)
            for n in range(B):
                sp.wait_ge(y_done, 2 * n + 2)
                sp.dma_start(out_v[:, 2 * n:2 * n + 2, :], y_out[:, 2 * n:2 * n + 2, :]).then_inc(stored, 16)
            sp.wait_ge(stored, 16 * (TB // 2))

        @blk_ctx.gpsimd
        def _(pool):
            steps = [0]

            def step(ins):
                steps[0] += 1
                ins.then_inc(pool_step, 1)
                pool.wait_ge(pool_step, steps[0])

            nc.gpsimd.memset(ones_b[:], 1.0).then_inc(consts, 1)
            nc.gpsimd.memset(v_ones[:], 1.0).then_inc(consts, 1)
            nc.gpsimd.memset(expo[:], -0.5)
            nc.gpsimd.memset(negm_p[:], 0.0)
            nc.gpsimd.memset(mask_qk[:], 0.0)
            nc.gpsimd.memset(mask_kq[:], 0.0)
            step(nc.gpsimd.memset(ident_f[:], 0.0))
            nc.gpsimd.affine_select(out=mask_qk[:], in_=mask_qk[:], compare_op=ALU.is_ge, fill=MASKED,
                                    base=0, pattern=[[0, 2], [-1, P]], channel_multiplier=1)
            nc.gpsimd.affine_select(out=mask_kq[:], in_=mask_kq[:], compare_op=ALU.is_ge, fill=MASKED,
                                    base=0, pattern=[[0, 2], [1, P]], channel_multiplier=-1)
            step(nc.gpsimd.affine_select(out=ident_f[:], in_=ident_f[:], compare_op=ALU.not_equal, fill=1.0,
                                         base=0, pattern=[[-1, P]], channel_multiplier=1))
            nc.gpsimd.tensor_copy(ident[:], ident_f[:]).then_inc(consts, 1)
            for stack, row in ((stack_q, ROW_BIAS), (stack_k, ROW_MAX)):
                pool.dma_start(stack[row:row + 3, :].rearrange("p (a t) -> p a t", a=B * H // 4),
                               ones_b[:].unsqueeze(1).to_broadcast([3, B * H // 4, T])).then_inc(stack_const, 16)
            pool.dma_start(stack_k[ROW_BIAS:ROW_BIAS + 3, :].rearrange("p (b n) -> p b n", b=B),
                           alibi.unsqueeze(1).to_broadcast([3, B, H * S])).then_inc(stack_const, 16)

            pool.wait_ge(ctx_max, 1)
            nc.gpsimd.partition_all_reduce(sc[:, 1:2], sc[:, 0:1], P, bass.bass_isa.ReduceOp.max)\
                .then_inc(ctx_all, 1)
            pool.wait_ge(ld["x"], 16)
            pool.wait_ge(ld["bo"], 16)
            nc.gpsimd.tensor_tensor(out=x_res[:], in0=x_res[:],
                                    in1=bo[:].unsqueeze(1).to_broadcast([P, TB, D]),
                                    op=ALU.add).then_inc(xres_done, 1)
            pool.wait_ge(wsum, 2)
            step(nc.gpsimd.partition_all_reduce(sc[:, 4:6], sc[:, 2:4], P, bass.bass_isa.ReduceOp.add))
            step(nc.gpsimd.tensor_scalar(sc[:, 14:16], sc[:, 4:6], 1.0 / (D * F), 1e-5, ALU.mult, ALU.max))
            nc.gpsimd.tensor_scalar(sc[:, 16:18], sc[:, 14:16], 0.7, None, ALU.mult)
            nc.gpsimd.tensor_scalar(sc[:, 18:20], sc[:, 14:16], -0.7, None, ALU.mult)
            step(nc.gpsimd.tensor_tensor(out=sc[:, 22:23], in0=sc[:, 14:15], in1=sc[:, 14:15], op=ALU.mult))
            step(nc.gpsimd.tensor_tensor(out=sc[:, 23:24], in0=sc[:, 22:23], in1=sc[:, 15:16], op=ALU.mult))
            nc.gpsimd.tensor_scalar(sc[:, 24:25], sc[:, 23:24], H_SCALE ** -2, None, ALU.mult)\
                .then_inc(tern_done, 1)

            def rstds(n):
                wait_apart(pool, aggr_done, 2 * n + 2)
                side = n % 2 if isinstance(n, int) and n >= B else 0
                nc.gpsimd.tensor_scalar(ve[:, side, :], mv[:, side, :, 1], LN_EPS, None, ALU.add)\
                    .then_inc(ve_done, 1)
                pool.wait_ge(ve_done, n + 1)
                nc.gpsimd.tensor_tensor(out=rstd[:, side, :], in0=ve[:, side, :], in1=expo[:],
                                        op=ALU.pow).then_inc(rstd_done, 1)

            def add_mask(b):
                pool.wait_ge(x1_done, 2 * b + 2)
                nc.gpsimd.tensor_tensor(out=x1m[:, 2 * b:2 * b + 2, :], in0=x1[:, 2 * b:2 * b + 2, :],
                                        in1=maskb[:, b, :].unsqueeze(1).to_broadcast([P, 2, D]),
                                        op=ALU.add).then_inc(x1m_done, 1)

            for n in range(B):
                pool.wait_ge(kv_scaled, n + 1)
                k2 = kv_ctx[:, 2 * n:2 * n + 2, :]
                nc.gpsimd.tensor_scalar(k2, k2, FP8_MAX, -FP8_MAX, ALU.min, ALU.max).then_inc(kv_clipped, 1)

            def round_context(n):
                pool.wait_ge(kv_magic, n + 1)
                k2, m2 = kv_ctx[:, 2 * n:2 * n + 2, :], magic[:, 2 * n:2 * n + 2, :]
                step(nc.gpsimd.tensor_tensor(out=k2, in0=k2, in1=m2, op=ALU.add))
                nc.gpsimd.tensor_tensor(out=kv_q[:, 2 * n:2 * n + 2, :], in0=k2, in1=m2, op=ALU.subtract)\
                    .then_inc(kvq_done, 1)

            def body(b, prev, nxt):
                for p in range(PAIRS):
                    if not nxt and p % 2 == 1:
                        round_context(p // 2)
                if prev:
                    rstds(b - 1)

            body(0, False, True)
            with pool.Fori(1, B - 1) as b:
                body(b, True, True)
            body(B - 1, True, False)
            pool.wait_ge(ld["mask"], 16)
            for n in range(B - 1):
                add_mask(n)
            rstds(B - 1)
            pool.wait_ge(x_max, 1)
            nc.gpsimd.partition_all_reduce(sc[:, 11:12], sc[:, 10:11], P, bass.bass_isa.ReduceOp.max)\
                .then_inc(x_all, 1)
            add_mask(B - 1)
            for n in range(B, 3 * B):
                rstds(n)

        @blk_ctx.scalar
        def _(act):
            act.dma_start(bqk[:], b_qk).then_inc(ld["bqk"], 16)
            act.dma_start(wv[:], w_v.rearrange("(c p) n -> p c n", p=P)).then_inc(ld["wv"], 16)
            act.dma_start(bv[:], b_v.partition_broadcast(P)).then_inc(ld["bv"], 16)
            act.dma_start(kv_ctx[:], ctx_in.rearrange("b (c p) n -> p (b c) n", p=P)).then_inc(ld["ctx"], 16)
            act.dma_start(wfc[:], w_fc.rearrange("(c p) n -> p c n", p=P)).then_inc(ld["wfc"], 16)
            act.dma_start(wpj[:], w_proj.rearrange("(c p) n -> p c n", p=P)).then_inc(ld["wpj"], 16)

            act.wait_ge(bq_done, 1)

            def qk_first(n):
                half, j = units[n]
                act.wait_ge(qk_mm, n + 1)
                wait(act, qk_r1, n - 1)
                nc.scalar.activation(qk_t[:, n % 2, :], ps[:, 4 + n % 4, :], ACT.Identity, bias=bqk[:, j:j + 1],
                                     scale=HD ** -0.5 if j < 2 else 1.0).then_inc(qk_f32, 1)
                act.wait_ge(qk_f32, n + 1)
                nc.scalar.activation(unit_part(n, 0), qk_t[:, n % 2, :].rearrange("p (b t) -> p b t", b=2),
                                     ACT.Copy).then_inc(qk_p0, 1)

            def sum_weights(w, col):
                nc.scalar.activation(pT[:].rearrange("p a n -> p (a n)")[:, 0:FC * D],
                                     w[:].rearrange("p a n -> p (a n)"), ACT.Abs,
                                     accum_out=sc[:, col:col + 1]).then_inc(wsum, 1)

            for n in range(4):
                qk_first(n)
            act.wait_ge(ld["wfc"], 16)
            sum_weights(wfc, 2)
            act.wait_ge(ld["wpj"], 16)
            act.wait_ge(wsum, 1)
            sum_weights(wpj, 3)
            for n in range(4, 8):
                qk_first(n)
            act.wait_ge(ctx_scaled, 1)
            for n in range(B):
                nc.scalar.activation(kv_ctx[:, 2 * n:2 * n + 2, :], kv_ctx[:, 2 * n:2 * n + 2, :], ACT.Copy,
                                     scale=sc[:, 8:9]).then_inc(kv_scaled, 1)

            def exps(b, p):
                for i in (2 * p, 2 * p + 1):
                    act.wait_ge(st_mm, b * H + i + 1)
                    if i % 4 == 0:
                        wait(act, pv_mm, b * GROUPS + i // 4 - 1)
                    nc.scalar.activation(pT[:, i % P_SLOTS, :], ps[:, BANK_ST + i % 2, 0:TRI], ACT.Exp)\
                        .then_inc(exp_done, 1)

            def copy_o(b, i):
                act.wait_ge(pv_mm, b * GROUPS + 2 * i + 2)
                wait(act, ot_mm, b * 2)
                nc.scalar.activation(o_raw[:, 2 * i:2 * i + 2, :].rearrange("p g q -> p (g q)"),
                                     ps[:, BANK_O, :], ACT.Copy).then_inc(o_copied, 1)

            def copy_oT(b):
                act.wait_ge(oT_mm, b + 1)
                wait(act, y_mm, b)
                nc.scalar.activation(oT[:].rearrange("p c q -> p (c q)"), ps[:, BANK_Y, :], ACT.Copy)\
                    .then_inc(oT_done, 1)

            def send_max(b, half):
                act.wait_ge(mT_done, 2 * b + half + 1)
                act.dma_start(stack_q[ROW_MAX:ROW_MAX + 3, cols(b, HC * half, 0, HC * S)], negm_T[:, half, :])\
                    .then_inc(mrows, 16)

            def copy_values(b):
                wait(act, pv_mm, b * GROUPS)
                nc.scalar.activation(v_ones[:, :, :, 0:HD],
                                     v_nat[:, blocks(b), :].rearrange("p k (h d) -> p k h d", h=H), ACT.Copy)\
                    .then_inc(vb_done, 1)

            def body(b, prev, nxt):
                for p in range(PAIRS):
                    exps(b, p)
                    if p == 0 and prev:
                        copy_o(b - 1, 1)
                    if p == 2:
                        send_max(b, 1)
                        copy_values(b)
                    if p == 4:
                        copy_o(b, 0)
                        if prev:
                            copy_oT(b - 1)
                    if p == 6 and nxt:
                        send_max(b + 1, 0)

            send_max(0, 0)
            act.wait_ge(v_done, 4)
            act.wait_ge(consts, 2)
            body(0, False, True)
            with act.Fori(1, B - 1) as b:
                body(b, True, True)
            body(B - 1, True, False)
            copy_o(B - 1, 1)
            copy_oT(B - 1)

            act.wait_ge(xs_done, 1)
            for n in range(B):
                nc.scalar.activation(xy[:, 2 * n:2 * n + 2, :], x1[:, 2 * n:2 * n + 2, :], ACT.Copy,
                                     scale=sc[:, 12:13]).then_inc(x_scaled, 1)
            def x2_high(n):
                act.wait_ge(x2T_mm, n + 1)
                nc.scalar.activation(x2_hi[:, :, n * S:(n + 1) * S],
                                     ps[:, 4 + n % 2, :].rearrange("p (c t) -> p c t", c=DC), ACT.Copy)\
                    .then_inc(x2hi_done, 1)

            def hidden(n):
                half, hc = divmod(n, FC)
                act.wait_ge(f1_mm, n + 1)
                wait(act, hs_done, n - 1)
                nc.scalar.activation(hu[:, n % 2, :], ps[:, F1_BANKS[n % 4], :], ACT.Relu, scale=H_SCALE)\
                    .then_inc(hu_done, 1)
                act.wait_ge(hu_done, n + 1)
                nc.scalar.activation(h_hi[:, hc, half * HALF:(half + 1) * HALF], hu[:, n % 2, :], ACT.Square)\
                    .then_inc(hhi_done, 1)

            for n in range(B):
                x2_high(n)
                if n == 1:
                    for m in range(3):
                        hidden(m)
            for n in range(3, 2 * FC):
                hidden(n)

        @blk_ctx.vector
        def _(dve):
            v = nc.vector
            steps = [0]

            def step(ins):
                steps[0] += 1
                ins.then_inc(dve_step, 1)
                dve.wait_ge(dve_step, steps[0])

            dve.wait_ge(ld["bqk"], 16)
            v.tensor_scalar(bqk[:, 0:2], bqk[:, 0:2], HD ** -0.5, None, ALU.mult).then_inc(bq_done, 1)

            def qk_parts(n):
                t3, r3 = (a[:, n % 2, :].rearrange("p (b t) -> p b t", b=2) for a in (qk_t, qk_r))
                dve.wait_ge(qk_p0, n + 1)
                v.tensor_tensor(out=r3, in0=t3, in1=unit_part(n, 0), op=ALU.subtract).then_inc(qk_r1, 1)
                dve.wait_ge(qk_r1, n + 1)
                v.tensor_copy(unit_part(n, 1), r3).then_inc(qk_p1, 1)
                dve.wait_ge(qk_p1, n + 1)
                v.tensor_tensor(out=unit_part(n, 2), in0=r3, in1=unit_part(n, 1), op=ALU.subtract)\
                    .then_inc(qk_p2, 1)

            def values_out(n):
                dve.wait_ge(v_mm, n + 1)
                if n == 0:
                    dve.wait_ge(ld["bv"], 16)
                v.tensor_tensor(out=v_nat[:, 2 * n:2 * n + 2, :],
                                in0=ps[:, n, :].rearrange("p (k n) -> p k n", k=2),
                                in1=bv[:].unsqueeze(1).to_broadcast([P, 2, D]), op=ALU.add)\
                    .then_inc(v_done, 1)

            def fp8_scale(amax, scale, inverse):
                step(v.tensor_scalar(sc[:, 20:21], amax, FP8_EPS, None, ALU.max))
                step(v.reciprocal(sc[:, 21:22], sc[:, 20:21]))
                v.tensor_scalar(inverse, sc[:, 20:21], 1.0 / FP8_MAX, None, ALU.mult)
                return v.tensor_scalar(scale, sc[:, 21:22], FP8_MAX, None, ALU.mult)

            def rounding(dst, y):
                step(v.tensor_scalar(dst.bitcast(I32), y.bitcast(I32), EXPONENT, None, ALU.bitwise_and))
                return v.tensor_scalar(dst, dst, FP8_SMALLEST, 1.5 * 2.0 ** 20, ALU.max, ALU.mult)

            for n in range(4):
                qk_parts(n)
            dve.wait_ge(ld["ctx"], 16)
            v.tensor_reduce(sc[:, 0:1], kv_ctx[:].rearrange("p a n -> p (a n)"), AX.X, ALU.max,
                            apply_absolute_value=True).then_inc(ctx_max, 1)
            for n in range(TB // 2):
                values_out(n)
            dve.wait_ge(ctx_all, 1)
            fp8_scale(sc[:, 1:2], sc[:, 8:9], sc[:, 9:10]).then_inc(ctx_scaled, 1)

            def row_max(b, p):
                dve.wait_ge(smax_mm, b * PAIRS + p + 1)
                if p in (1, 5):
                    wait(dve, mT_mm, 2 * b + p // 5)
                if p % 4 == 0:
                    wait(dve, mparts, 6 * (2 * b + p // 4))
                bank = BANK_SM + 2 * (p % 2)
                v.tensor_reduce(negm3[:, 2 * p:2 * p + 2, :],
                                ps[:, bank:bank + 2, 0:TRI].rearrange("p e (a k) -> p e a k", k=P), AX.X, ALU.max,
                                negate=True).then_inc(smax_red, 1)

            def max_parts(b, half):
                done = 6 * (2 * b + half)
                dve.wait_ge(smax_red, b * PAIRS + 4 * half + 4)
                wait(dve, mT_mm, 2 * b + half - 1)
                if isinstance(b, int) and b == 0 and half == 0:
                    dve.wait_ge(consts, 3)
                three = negm3[:, HC * half:HC * (half + 1), :]
                negm, (r0, r1_), (p0, p1, p2) = (three[:, :, 0:2].rearrange("p h k -> p k h"),
                                                 (negm_r[:, 0], negm_r[:, 1]),
                                                 (negm_p[:, half, :, part, :] for part in range(3)))
                v.tensor_tensor(out=three[:, :, 1], in0=three[:, :, 1], in1=three[:, :, 2], op=ALU.min)\
                    .then_inc(mparts, 1)
                dve.wait_ge(mparts, done + 1)
                v.tensor_copy(p0, negm).then_inc(mparts, 1)
                dve.wait_ge(mparts, done + 2)
                v.tensor_tensor(out=r0, in0=negm, in1=p0, op=ALU.subtract).then_inc(mparts, 1)
                dve.wait_ge(mparts, done + 3)
                v.tensor_copy(p1, r0).then_inc(mparts, 1)
                dve.wait_ge(mparts, done + 4)
                v.tensor_tensor(out=r1_, in0=r0, in1=p1, op=ALU.subtract).then_inc(mparts, 1)
                dve.wait_ge(mparts, done + 5)
                v.tensor_copy(p2, r1_).then_inc(mparts, 1)

            def copy_max(b, half):
                dve.wait_ge(mT_mm, 2 * b + half + 1)
                wait(dve, mrows, 16 * (2 * b + half - 1))
                v.tensor_copy(negm_T[:, half, :], ps[0:3 * HC, MT_BANK[half], TRI:512].bitcast(BF16))\
                    .then_inc(mT_done, 1)

            def normalise(b, i, bank=BANK_Y):
                dve.wait_ge(ot_mm, 2 * b + i + 1)
                wait(dve, oT_mm, b)
                heads = ps[:, bank, :].rearrange("p (h d) -> p h d", d=2 * HD)
                v.reciprocal(rden[:, i, :].unsqueeze(2), heads[:, :, HD:HD + 1]).then_inc(rden_done, 1)
                dve.wait_ge(rden_done, 2 * b + i + 1)
                for c in range(DC):
                    last = v.tensor_tensor(out=o_nrm[:, i, c * P:(c + 1) * P].rearrange("p (h d) -> p h d", d=HD),
                                           in0=heads[:, c:H:DC, 0:HD],
                                           in1=rden[:, i, c:H:DC].unsqueeze(2).to_broadcast([P, HC, HD]),
                                           op=ALU.mult)
                last.then_inc(o_done, 1)

            def add_residual(b):
                dve.wait_ge(y_mm, b + 1)
                v.tensor_tensor(out=r1[:, blocks(b), :], in0=ps[:, BANK_Y, :].rearrange("p (k n) -> p k n", k=2),
                                in1=x_res[:, blocks(b), :], op=ALU.add).then_inc(r1_done, 1)
                statistics(lambda i: r1[:, block(b, i), :], b, 0, r1_done, b + 1)

            def statistics(rows, n, parity, summed, count):
                wait_apart(dve, summed, count)
                wait(dve, aggr_done, 2 * n)

                for i in range(2):
                    v.bn_stats(stats[:, i, :], rows(i)).then_inc(stat_done, 1)
                for i in range(2):
                    wait_apart(dve, stat_done, 2 * n + i + 1)
                    v.bn_aggr(mv[:, parity, i, :], stats[:, i, :]).then_inc(aggr_done, 1)

            def first_norm(b):
                dve.wait_ge(rstd_done, b + 1)
                for i in range(2):
                    v.tensor_scalar(x1[:, block(b, i), :], r1[:, block(b, i), :], mv[:, 0, i, 0:1],
                                    rstd[:, 0, i:i + 1], ALU.subtract, ALU.mult).then_inc(x1_done, 1)
                dve.wait_ge(x1_done, 2 * b + 2)
                v.tensor_reduce(amax[:, b:b + 1] if isinstance(b, int) else amax[:, bass.ds(b, 1)],
                                x1[:, blocks(b), :], AX.XY, ALU.max, apply_absolute_value=True).then_inc(b_max, 1)

            def ternarise(i):
                w2, wt2 = ((wfc, wfc_t), (wpj, wpj_t))[i]
                w2, wt2 = w2[:].rearrange("p a n -> p (a n)"), wt2[:].rearrange("p a n -> p (a n)")
                dve.wait_ge(tern_done, 1 + i)
                step(v.tensor_scalar(w_low[:], w2, sc[:, 18 + i:19 + i], None, ALU.is_lt))
                v.scalar_tensor_tensor(wt2, w2, sc[:, 16 + i:17 + i], w_low[:], ALU.is_gt, ALU.subtract)\
                    .then_inc(tern_done, 1)

            def context_magic():
                for n in range(B):
                    dve.wait_ge(kv_clipped, n + 1)
                    rounding(magic[:, 2 * n:2 * n + 2, :], kv_ctx[:, 2 * n:2 * n + 2, :]).then_inc(kv_magic, 1)

            def body(b, prev, nxt):
                for p in range(PAIRS):
                    if prev and p in (2, 3):
                        normalise(b - 1, p - 2)
                    if prev and p == 7:
                        first_norm(b - 1)
                    if nxt:
                        row_max(b + 1, p)
                    if p == 1:
                        copy_max(b, 1)
                    if nxt and p == 3:
                        max_parts(b + 1, 0)
                    if nxt and p == 5:
                        copy_max(b + 1, 0)
                    if nxt and p == 7:
                        max_parts(b + 1, 1)
                    if prev and p == 5:
                        add_residual(b - 1)
                    if not nxt and p == 1:
                        context_magic()
                    if not nxt and p in (4, 6):
                        ternarise(p // 2 - 2)

            for p in range(PAIRS):
                row_max(0, p)
                if p == 3:
                    max_parts(0, 0)
                if p == 5:
                    copy_max(0, 0)
                if p % 2 == 0:
                    qk_parts(4 + p // 2)
            max_parts(0, 1)
            body(0, False, True)
            dve.wait_ge(xres_done, 1)
            with dve.Fori(1, B - 1) as b:
                body(b, True, True)
            body(B - 1, True, False)
            normalise(B - 1, 0)
            normalise(B - 1, 1)
            add_residual(B - 1)
            first_norm(B - 1)

            dve.wait_ge(b_max, B)
            v.tensor_reduce(sc[:, 10:11], amax[:], AX.X, ALU.max).then_inc(x_max, 1)
            dve.wait_ge(x_all, 1)
            fp8_scale(sc[:, 11:12], sc[:, 12:13], sc[:, 13:14]).then_inc(xs_done, 1)
            dve.wait_ge(xs_done, 1)
            step(v.tensor_tensor(out=sc[:, 25:26], in0=sc[:, 13:14], in1=sc[:, 9:10], op=ALU.mult))

            def unit(a, n):
                return a[:, 2 * n:2 * n + 2, :].rearrange("p a n -> p (a n)")

            def quantise(n):
                dve.wait_ge(x_scaled, n + 1)
                m = qe[:, n % 2, :]
                wait(dve, xq_done, n - 1)
                step(rounding(m, unit(xy, n)))
                step(v.scalar_tensor_tensor(unit(xy, n), unit(xy, n), FP8_MAX, m, ALU.min, ALU.add))
                v.tensor_tensor(out=unit(x_q, n), in0=unit(xy, n), in1=m, op=ALU.subtract).then_inc(xq_done, 1)

            def turned(n):
                dve.wait_ge(xqT_mm, n + 1)
                v.tensor_scalar(x_qT[:, :, n * S:(n + 1) * S],
                                ps[:, n % 2, 0:S].bitcast(BF16).rearrange("p (c t) -> p c t", c=DC),
                                -FP8_MAX, None, ALU.max).then_inc(xqT_done, 1)

            def cross_residual(n):
                dve.wait_ge(xa_mm, n + 1)
                dve.wait_ge(x1m_done, n + 1)
                v.scalar_tensor_tensor(unit(r1, n), ps[:, 2 + n % 2, :], sc[:, 25:26], unit(x1m, n),
                                       ALU.mult, ALU.add).then_inc(r2_done, 1)
                statistics(lambda i: r1[:, 2 * n + i, :], B + n, (B + n) % 2, r2_done, n + 1)

            def norm(dst, n, u, signal):
                dve.wait_ge(rstd_done, u + 1)
                for i in range(2):
                    k = 2 * n + i
                    v.tensor_scalar(dst[:, k, :], r1[:, k, :], mv[:, u % 2, i, 0:1], rstd[:, u % 2, i:i + 1],
                                    ALU.subtract, ALU.mult).then_inc(signal, 1)

            def x2_low(n):
                dve.wait_ge(x2hi_done, n + 1)
                v.tensor_tensor(out=x2_lo[:, :, n * S:(n + 1) * S],
                                in0=ps[:, 4 + n % 2, :].rearrange("p (c t) -> p c t", c=DC),
                                in1=x2_hi[:, :, n * S:(n + 1) * S], op=ALU.subtract).then_inc(x2lo_done, 1)

            def hidden(n):
                half, hc = divmod(n, FC)
                dve.wait_ge(hu_done, n + 1)
                wait(dve, hlo_done, n - 1)
                v.tensor_tensor(out=hs[:, n % 2, :], in0=hu[:, n % 2, :], in1=hu[:, n % 2, :], op=ALU.mult)\
                    .then_inc(hs_done, 1)
                dve.wait_ge(hs_done, n + 1)
                dve.wait_ge(hhi_done, n + 1)
                v.tensor_tensor(out=h_lo[:, hc, half * HALF:(half + 1) * HALF], in0=hs[:, n % 2, :],
                                in1=h_hi[:, hc, half * HALF:(half + 1) * HALF], op=ALU.subtract)\
                    .then_inc(hlo_done, 1)

            def last_residual(n):
                dve.wait_ge(f2_mm, n + 1)
                v.scalar_tensor_tensor(unit(r1, n), ps[:, 2 + n, :], sc[:, 24:25], unit(x2, n),
                                       ALU.mult, ALU.add).then_inc(r3_done, 1)
                statistics(lambda i: r1[:, 2 * n + i, :], 2 * B + n, (2 * B + n) % 2, r3_done, n + 1)

            for n in range(B + 3):
                if n < B:
                    quantise(n)
                if 1 <= n < B + 1:
                    turned(n - 1)
                if 2 <= n < B + 2:
                    cross_residual(n - 2)
                if n >= 3:
                    norm(x2, n - 3, B + n - 3, x2_done)
            dve.wait_ge(tern_done, 1)
            for n in range(B):
                x2_low(n)
                if n == 1:
                    for m in range(3):
                        hidden(m)
            for n in range(3, 2 * FC):
                hidden(n)
            for n in range(B):
                last_residual(n)
                if n > 0:
                    norm(y_out, n - 1, 2 * B + n - 1, y_done)
            norm(y_out, B - 1, 3 * B - 1, y_done)

        @blk_ctx.tensor
        def _(pe):
            mm = nc.tensor.matmul
            pe.wait_ge(ld["wqk"], 16)

            def project_qk(n):
                half, j = units[n]
                if j == 0:
                    pe.wait_ge(ld[f"xT{half}"], 16)
                wait(pe, qk_f32, n - 3)
                for c in range(DC):
                    last = mm(ps[:, 4 + n % 4, :], wqk[:, c, j, :], xT[:, c, half * HALF:(half + 1) * HALF],
                              start=(c == 0), stop=(c == DC - 1))
                last.then_inc(qk_mm, 1)
            for n in range(4):
                project_qk(n)
            pe.wait_ge(ld["wv"], 16)
            pe.wait_ge(ld["xT1"], 16)
            for n in range(TB // 2):
                for i in range(2):
                    k = 2 * n + i
                    for c in range(DC):
                        last = mm(ps[:, n, i * D:(i + 1) * D], xT[:, c, k * P:(k + 1) * P], wv[:, c, :],
                                  start=(c == 0), stop=(c == DC - 1))
                last.then_inc(v_mm, 1)

            def score_max(b, p):
                wait(pe, smax_red, b * PAIRS + p - 1)
                if p == 7:
                    pe.wait_ge(mT_done, 2 * b + 1)
                if p == 3:
                    wait(pe, mT_done, 2 * b)
                for e in range(2):
                    i, bank = 2 * p + e, BANK_SM + 2 * (p % 2) + e
                    mm(diag(bank), ident[:], mask_qk[:], start=True, stop=False, skip_group_check=True)
                    mm(ps[:, bank, 0:P], stack_q[0:ROW_MAX, cols(b, i, 0, P)], stack_k[0:ROW_MAX, cols(b, i, 0, P)],
                       start=False, stop=False, skip_group_check=True)
                    last = mm(ps[:, bank, P:TRI], stack_q[0:ROW_MAX, cols(b, i, P, P)],
                              stack_k[0:ROW_MAX, cols(b, i, 0, S)], start=False, stop=True, skip_group_check=True)
                last.then_inc(smax_mm, 1)

            def scores(b, p):
                if p % 4 == 0:
                    pe.wait_ge(mrows, 16 * (2 * b + p // 4 + 1))
                for i in (2 * p, 2 * p + 1):
                    wait(pe, exp_done, b * H + i - 1)
                    bank = BANK_ST + i % 2
                    mm(diag(bank), ident[:], mask_kq[:], start=True, stop=False, skip_group_check=True)
                    mm(ps[:, bank, 0:S], stack_k[0:ROWS, cols(b, i, 0, P)], stack_q[0:ROWS, cols(b, i, 0, S)],
                       start=False, stop=False, skip_group_check=True)
                    mm(ps[:, bank, S:TRI], stack_k[0:ROWS, cols(b, i, P, P)], stack_q[0:ROWS, cols(b, i, P, P)],
                       start=False, stop=True, skip_group_check=True).then_inc(st_mm, 1)

            def max_to_rows(b, half):
                pe.wait_ge(mparts, 6 * (2 * b + half + 1))
                spare = ps[:, MT_BANK[half], TRI:512]
                for i in range(2):
                    last = nc.tensor.transpose(spare[:, i * P // 2:(i + 1) * P // 2].bitcast(BF16),
                                               negm_p[:, half, i, :, :].rearrange("p a h -> p (a h)"), ident[:])
                last.then_inc(mT_mm, 1)

            def values(b, g):
                pe.wait_ge(exp_done, b * H + 4 * g + 4)
                if g == 0:
                    pe.wait_ge(vb_done, b + 1)
                if g % 2 == 0:
                    wait(pe, o_copied, 2 * b + g // 2)
                o = (g % 2) * S
                for k in range(2):
                    for j in range(4):
                        prob = pT[:, (4 * g + j) % P_SLOTS, :]
                        last = mm(ps[32 * j:32 * j + 32, BANK_O, o + k * P:o + S],
                                  v_ones[:, k, head(4 * g + j), :],
                                  prob[:, 0:S] if k == 0 else prob[:, S:TRI], start=(k == 0), stop=(k == 1),
                                  skip_group_check=True)
                last.then_inc(pv_mm, 1)

            def queries_down(b, i):
                if i == 0:
                    pe.wait_ge(o_copied, 2 * b + 2)
                    if isinstance(b, int) and b == B - 1:
                        pe.wait_ge(r1_done, b)
                else:
                    pe.wait_ge(o_done, 2 * b + 1)
                for g in range(GROUPS):
                    last = nc.tensor.transpose(ps[:, BANK_Y, g * P:(g + 1) * P],
                                               o_raw[:, g, i * P:(i + 1) * P], ident_f[:])
                last.then_inc(ot_mm, 1)

            def features_down(b):
                pe.wait_ge(o_done, 2 * b + 2)
                for i in range(2):
                    for c in range(DC):
                        last = nc.tensor.transpose(ps[:, BANK_Y, c * S + i * P:c * S + (i + 1) * P],
                                                   o_nrm[:, i, c * P:(c + 1) * P], ident_f[:])
                last.then_inc(oT_mm, 1)

            def project(b):
                pe.wait_ge(oT_done, b + 1)
                for i in range(2):
                    for c in range(DC):
                        last = mm(ps[:, BANK_Y, i * D:(i + 1) * D], oT[:, c, i * P:(i + 1) * P], wo[:, c, :],
                                  start=(c == 0), stop=(c == DC - 1))
                last.then_inc(y_mm, 1)

            def body(b, prev, nxt):
                for p in range(PAIRS):
                    scores(b, p)
                    if p == 5 and prev:
                        project(b - 1)
                    if nxt:
                        score_max(b + 1, p)
                    if p == 1:
                        max_to_rows(b, 1)
                    if p == 5 and nxt:
                        max_to_rows(b + 1, 0)
                    if p in (1, 2) and prev:
                        queries_down(b - 1, p - 1)
                    if p == 3 and prev:
                        features_down(b - 1)
                    if p == 0 and prev:
                        values(b - 1, 3)
                    if p in (2, 4, 6):
                        values(b, p // 2 - 1)

            pe.wait_ge(consts, 3)
            pe.wait_ge(stacked[0], 12 * 16)
            pe.wait_ge(stack_const, 3 * 16)
            pe.wait_ge(v_done, 4)
            for p in range(PAIRS):
                score_max(0, p)
                if p % 2 == 0:
                    project_qk(4 + p // 2)
                if p == 5:
                    max_to_rows(0, 0)
            pe.wait_ge(qk_f32, 8)
            pe.wait_ge(stacked[1], 12 * 16)
            pe.wait_ge(ld["wo"], 16)
            body(0, False, True)
            pe.wait_ge(stacked[2], 12 * 16)
            pe.wait_ge(stacked[3], 12 * 16)
            with pe.Fori(1, B - 1) as b:
                body(b, True, True)
            body(B - 1, True, False)
            values(B - 1, 3)
            queries_down(B - 1, 0)
            queries_down(B - 1, 1)
            features_down(B - 1)
            project(B - 1)

            pe.wait_ge(kvq_done, 4)
            pe.wait_ge(r1_done, B)

            def turn_values(n):
                pe.wait_ge(xq_done, n + 1)
                wait(pe, xqT_done, n - 1)
                tr = ps[:, n % 2, 0:S].bitcast(BF16)
                for i in range(2):
                    for c in range(DC):
                        last = nc.tensor.transpose(tr[:, c * S + i * P:c * S + (i + 1) * P],
                                                   x_q[:, 2 * n + i, c * P:(c + 1) * P], ident[:])
                last.then_inc(xqT_mm, 1)

            def cross(n):
                pe.wait_ge(xqT_done, n + 1)
                wait(pe, r2_done, n - 1)
                for i in range(2):
                    k = 2 * n + i
                    for c in range(DC):
                        last = mm(ps[:, 2 + n % 2, i * D:(i + 1) * D], x_qT[:, c, k * P:(k + 1) * P],
                                  kv_q[:, 2 * n + c, :], start=(c == 0), stop=(c == DC - 1))
                last.then_inc(xa_mm, 1)

            def turn_x2(n):
                pe.wait_ge(x2_done, 2 * n + 2)
                wait(pe, x2lo_done, n - 1)
                for i in range(2):
                    for c in range(DC):
                        last = nc.tensor.transpose(ps[:, 4 + n % 2, c * S + i * P:c * S + (i + 1) * P],
                                                   x2[:, 2 * n + i, c * P:(c + 1) * P], ident_f[:])
                last.then_inc(x2T_mm, 1)

            def hidden(n):
                half, hc = divmod(n, FC)
                if hc == 0:
                    pe.wait_ge(x2lo_done, 2 * half + 2)
                wait(pe, hu_done, n - 3)
                for c in range(DC):
                    for part in (x2_hi, x2_lo):
                        last = mm(ps[:, F1_BANKS[n % 4], :], wfc_t[:, c, hc * P:(hc + 1) * P],
                                  part[:, c, half * HALF:(half + 1) * HALF],
                                  start=(c == 0 and part is x2_hi), stop=(c == DC - 1 and part is x2_lo))
                last.then_inc(f1_mm, 1)

            def back(n):
                pe.wait_ge(hlo_done, FC * (n // 2 + 1))
                for i in range(2):
                    k = 2 * n + i
                    for hc in range(FC):
                        for part in (h_hi, h_lo):
                            last = mm(ps[:, 2 + n, i * D:(i + 1) * D], part[:, hc, k * P:(k + 1) * P],
                                      wpj_t[:, hc, :], start=(hc == 0 and part is h_hi),
                                      stop=(hc == FC - 1 and part is h_lo))
                last.then_inc(f2_mm, 1)

            for n in range(B + 3):
                if n < B:
                    turn_values(n)
                if 1 <= n < B + 1:
                    cross(n - 1)
                if n >= 3:
                    turn_x2(n - 3)
                if n == 4:
                    pe.wait_ge(tern_done, 3)
                    for m in range(3):
                        hidden(m)
            for n in range(3, 2 * FC):
                hidden(n)
            pe.wait_ge(r2_done, 4)
            for n in range(B):
                back(n)


def kernel(x, ctx_2048, mask_Bx1xS2_ff0, L0_attn_Wqkv, L0_attn_b_qkv, L0_attn_Wout, L0_attn_b_out,
           L0_ffn_w_fc, L0_ffn_w_proj):
    import numpy as _np
    import concourse.bacc as _bacc
    from concourse import mybir as _mybir
    from concourse.bass_utils import run_bass_kernel_spmd as _run

    x, ctx, mask, wqkv, bqkv, wout, bout, wfc, wproj = (_np.asarray(a) for a in (
        x, ctx_2048, mask_Bx1xS2_ff0, L0_attn_Wqkv, L0_attn_b_qkv, L0_attn_Wout, L0_attn_b_out,
        L0_ffn_w_fc, L0_ffn_w_proj))
    w_qk = wqkv[:2 * D].reshape(4, HC, HD, D).transpose(3, 0, 2, 1).reshape(D, 4 * P)
    b_qk = bqkv[:2 * D].reshape(4, HC, HD).transpose(2, 1, 0).reshape(P, 4)
    slopes = 1.0 / 2.0 ** (_np.arange(1, H + 1, dtype=_np.float32) * _np.float32(8.0 / H))
    alibi = _np.arange(1 - S, 1, dtype=_np.float32)[None, :] * slopes.astype(_np.float32)[:, None]
    alibi = alibi.reshape(DC, HC, S).transpose(1, 0, 2).reshape(H * S)
    alibi_parts = _np.zeros((3, H * S), dtype=_mybir.dt.np(BF16))
    for part in range(3):
        alibi_parts[part] = alibi
        alibi = alibi - alibi_parts[part].astype(_np.float32)
    arrays = {
        "x_nat": x, "x_tr": x.reshape(T, D).T, "ctx_in": ctx, "mask_in": mask, "w_qk": w_qk, "b_qk": b_qk,
        "w_v": wqkv[2 * D:].T, "b_v": bqkv[2 * D:], "w_out": wout.T, "b_out": bout,
        "w_fc": wfc.T, "w_proj": wproj.T, "alibi": alibi_parts,
    }
    arrays = {n: _np.ascontiguousarray(a) for n, a in arrays.items()}
    nc = _bacc.Bacc("TRN2", target_bir_lowering=False, num_devices=1)
    args = [nc.dram_tensor(n, a.shape, _mybir.dt.from_np(a.dtype), kind="ExternalInput").ap()
            for n, a in arrays.items()]
    y = nc.dram_tensor("y", (B, S, D), F32, kind="ExternalOutput").ap()
    decoder_kernel(nc, *args, y)
    r = _run(nc, [arrays], core_ids=[0])
    return r.results[0]["y"]
```

```python
from contextlib import ExitStack

import numpy as np

import concourse.bass as bass
from concourse import mybir

F32 = mybir.dt.float32
BF16 = mybir.dt.bfloat16
FP16 = mybir.dt.float16
I32 = mybir.dt.int32
ALU = mybir.AluOpType
ACT = mybir.ActivationFunctionType
AX = mybir.AxisListType

P = 128
B, S, D, H = 4, 256, 256, 16
HD = D // H
T = B * S
TB = T // P
DC = D // P
F = 640
FC = F // P
HALF = T // 2
HC = P // HD
PAIRS = H // 2
GROUPS = H // 4

PRODUCTS = [(0, 0), (0, 1), (1, 0), (1, 1), (0, 2), (2, 0)]
ROW_BIAS = HD * len(PRODUCTS)
ROW_MAX = ROW_BIAS + 3
ROWS = ROW_MAX + 3

TRI = P + 2 * P
MASKED = -1.0e9
LN_EPS = 1e-5
FP8_MAX = 448.0
FP8_EPS = 1e-12
EXPONENT = 0x7F800000
FP8_SMALLEST = 2.0 ** -6
H_SCALE = 0.25

BANK_SM, BANK_ST, BANK_O, BANK_Y = 0, 4, 6, 7
MT_BANK = (1, 3)
F1_BANKS = (6, 7, 0, 1)
LAST_BANKS = (5, 0)
WARM_START = 20
WARM_MAXIMA = 4
WARM_SCALE = 68
WARM_TURNED = 4
WARM_UNIT = 10
MAGIC_PAIRS = (2, 3)
RESIDUAL_AT = 3
EARLY = 4
P_SLOTS = 8


def decoder_kernel(nc, x_nat, x_tr, ctx_in, mask_in, w_qk, b_qk, w_v, b_v, w_out, b_out, w_fc, w_proj,
                   alibi, out):
    es = ExitStack()
    with es:
        def sb(name, shape, dt=F32):
            return es.enter_context(nc.sbuf_tensor(name, shape, dt))

        def sem(name):
            return es.enter_context(nc.semaphore(name))

        xT = sb("xT", [P, DC, T])
        x_res = sb("x_res", [P, TB, D])
        wqk = sb("wqk", [P, DC, 4, P])
        bqk = sb("bqk", [P, 4])
        wv = sb("wv", [P, DC, D])
        bv = sb("bv", [P, D])
        bo = sb("bo", [P, D])
        wo = sb("wo", [P, DC, D])
        wfc = sb("wfc", [P, DC, F])
        wpj = sb("wpj", [P, FC, D])
        wfc_t = sb("wfc_t", [P, DC, F], FP16)
        wpj_t = sb("wpj_t", [P, FC, D], FP16)
        w_low = sb("w_low", [P, FC * D], FP16)
        kv_ctx = sb("kv_ctx", [P, TB, D])
        kv_q = sb("kv_q", [P, TB, D], BF16)
        maskb = sb("maskb", [P, B, D])
        ones_b = sb("ones_b", [3, T], BF16)
        ident = sb("ident", [P, P], BF16)
        ident_f = sb("ident_f", [P, P])
        mask_qk = sb("mask_qk", [P, 2, P], BF16)
        mask_kq = sb("mask_kq", [P, 2, P], BF16)
        qk_t = sb("qk_t", [P, 2, HALF])
        qk_r = sb("qk_r", [P, 2, HALF])
        parts = sb("parts", [P, 3, 2, B, DC * S], BF16)
        stack_q = sb("stack_q", [P, B * H * S], BF16)
        stack_k = sb("stack_k", [P, B * H * S], BF16)
        v_nat = sb("v_nat", [P, TB, D])
        v_ones = sb("v_ones", [P, 2, H, 2 * HD])
        negm3 = sb("negm3", [P, H, 3])
        negm_r = sb("negm_r", [P, 2, 2, HC])
        negm_p = sb("negm_p", [P, 2, 2, P // HC, HC], BF16)
        negm_T = sb("negm_T", [3 * HC, 2, S], BF16)
        pT = sb("pT", [P, P_SLOTS, TRI])
        o_raw = sb("o_raw", [P, GROUPS, S])
        rden = sb("rden", [P, 2, H])
        o_nrm = sb("o_nrm", [P, 2, D])
        oT = sb("oT", [P, DC, S])
        r1 = x_res
        stats = sb("stats", [P, 2, 6])
        mv = sb("mv", [P, 2, 2, 2])
        ve = sb("ve", [P, 2, 2])
        rstd = sb("rstd", [P, 2, 2])
        nmean = sb("nmean", [P, 2, 2])
        nbias = sb("nbias", [P, 2, 2])
        expo = sb("expo", [P, 2])
        amax = sb("amax", [P, B])
        sc = sb("sc", [P, 32])
        qe = sb("qe", [P, 2, 2 * D])

        def over(buffer, at, shape, dt):
            n = int(np.prod(shape[1:])) * (2 if dt == F32 else 1)
            letters = "abc"[:len(shape) - 1]
            sizes = dict(zip(letters[1:], shape[2:]))
            flat = buffer[:] if len(buffer.shape) == 2 else buffer[:].rearrange("p a b c d -> p (a b c d)")
            return flat[:, at:at + n].bitcast(dt).rearrange(
                f"p ({' '.join(letters)}) -> p {' '.join(letters)}", **sizes)

        h_hi = over(stack_k, 0, [P, FC, T], FP16)
        h_lo = over(stack_k, FC * T, [P, FC, T], FP16)
        x_qT = over(stack_k, 2 * FC * T, [P, DC, T], BF16)
        x2_hi = over(stack_k, (2 * FC + DC) * T, [P, DC, T], FP16)
        x2_lo = over(stack_k, (2 * FC + 2 * DC) * T, [P, DC, T], FP16)
        x2 = over(parts, 0, [P, TB, D], F32)
        x1m = over(parts, 2 * TB * D, [P, TB, D], F32)
        y_out = over(parts, 4 * TB * D, [P, TB, D], F32)
        x1 = over(stack_q, 0, [P, TB, D], F32)
        x_q = over(stack_q, 2 * TB * D, [P, TB, D], BF16)
        hu, hs = qk_t, qk_r
        magic = xT[:].rearrange("p c (a n) -> p (c a) n", n=D)
        xy = kv_ctx
        ps = es.enter_context(nc.psum_tensor("ps", [P, 8, 512], F32))

        ld = {n: sem("ld_" + n) for n in (
            "xT0", "xT1", "wq0", "wqk", "bqk", "x", "wv", "bv", "bo", "wo", "wfc", "wpj", "ctx", "mask")}
        zeros, consts = sem("zeros"), sem("consts")
        pool_step = sem("pool_step")
        xres_done = sem("xres_done")
        bq_done = sem("bq_done")
        qk_mm, qk_f32, qk_p0, qk_r1, qk_p1, qk_p2 = (sem(n) for n in (
            "qk_mm", "qk_f32", "qk_p0", "qk_r1", "qk_p1", "qk_p2"))
        stacked = [sem(f"stacked_{b}") for b in range(B)]
        stack_ready = sem("stack_ready")
        stack_const = sem("stack_const")
        v_mm, v_done, vb_done = sem("v_mm"), sem("v_done"), sem("vb_done")
        smax_mm, smax_red, mparts, mT_mm, mT_done, mrows = (sem(n) for n in (
            "smax_mm", "smax_red", "mparts", "mT_mm", "mT_done", "mrows"))
        st_mm, exp_done, pv_mm, o_copied = (sem(n) for n in (
            "st_mm", "exp_done", "pv_mm", "o_copied"))
        ot_mm, rden_done, o_done, oT_mm, oT_done, y_mm, r1_done = (sem(n) for n in (
            "ot_mm", "rden_done", "o_done", "oT_mm", "oT_done", "y_mm", "r1_done"))
        stat_done, aggr_done = sem("stat_done"), sem("aggr_done")
        ve_done, pow_done, rstd_done = sem("ve_done"), sem("pow_done"), sem("rstd_done")
        x1_done, x1m_done = sem("x1_done"), sem("x1m_done")
        dve_step = sem("dve_step")
        ctx_max, ctx_all, x_max, x_all, xs_done = (sem(n) for n in (
            "ctx_max", "ctx_all", "x_max", "x_all", "xs_done"))
        wsum = sem("wsum")
        kvq_done, tern_done, ctx_scaled, kv_scaled, kv_magic = (sem(n) for n in (
            "kvq_done", "tern_done", "ctx_scaled", "kv_scaled", "kv_magic"))
        b_max, q_step, x_scaled = sem("b_max"), sem("q_step"), sem("x_scaled")
        xq_done, xqT_mm, xqT_done, xa_mm, r2_done = (sem(n) for n in (
            "xq_done", "xqT_mm", "xqT_done", "xa_mm", "r2_done"))
        x2_done, x2T_mm, x2hi_done, x2lo_done = (sem(n) for n in ("x2_done", "x2T_mm", "x2hi_done", "x2lo_done"))
        f1_mm, hu_done, hs_done, hhi_done, hlo_done, f2_mm, r3_done, y_done = (sem(n) for n in (
            "f1_mm", "hu_done", "hs_done", "hhi_done", "hlo_done", "f2_mm", "r3_done", "y_done"))
        stored = sem("stored")

        def wait(eng, s, value):
            if isinstance(value, int) and value <= 0:
                return
            eng.wait_ge(s, value)

        def wait_apart(eng, s, value):
            if isinstance(value, int):
                eng.wait_ge(s, value)
            else:
                value = eng.snap(eng.to_reg(value))
                eng.wait_ge(s, 1)
                eng.wait_ge(s, value)

        def cols(b, i, first, count):
            at = (b * H + i) * S + first
            return slice(at, at + count) if isinstance(b, int) else bass.ds(at, count)

        def blocks(b):
            return slice(2 * b, 2 * b + 2) if isinstance(b, int) else bass.ds(2 * b, 2)

        def block(b, i):
            return slice(2 * b + i, 2 * b + i + 1) if isinstance(b, int) else bass.ds(2 * b + i, 1)

        def diag(bank):
            return ps[:, bank, :].rearrange("p (a c) -> p a c", c=2 * P)[:, :, 0:P]

        units = [(half, j) for half in range(2) for j in range(4)]

        def unit_part(n, i):
            half, j = units[n]
            return parts[:, i, j // 2, 2 * half:2 * half + 2, (j % 2) * S:(j % 2 + 1) * S]

        def head(i):
            return HC * (i % 2) + i // 2

        blk_ctx = es.enter_context(nc.Block())

        @blk_ctx.sync
        def _(sp):
            xt_v = x_tr.rearrange("(c p) t -> p c t", p=P)
            wqk_v = w_qk.rearrange("(c p) (j n) -> p c j n", p=P, j=4)
            sp.dma_start(wqk[:, :, 0, :], wqk_v[:, :, 0, :]).then_inc(ld["wq0"], 16)
            sp.dma_start(xT[:, :, 0:HALF], xt_v[:, :, 0:HALF]).then_inc(ld["xT0"], 16)
            sp.dma_start(wqk[:, :, 1:4, :], wqk_v[:, :, 1:4, :]).then_inc(ld["wqk"], 16)
            sp.dma_start(xT[:, :, HALF:T], xt_v[:, :, HALF:T]).then_inc(ld["xT1"], 16)

            for b in range(B):
                for qk, stack in ((0, stack_q), (1, stack_k)):
                    for g, pair in sorted(enumerate(PRODUCTS), key=lambda product: product[1][qk]):
                        sp.wait_ge((qk_p0, qk_p1, qk_p2)[pair[qk]], 4 * (b // 2) + 2 * qk + 2)
                        sp.dma_start(stack[HD * g:HD * (g + 1), cols(b, 0, 0, H * S)],
                                     parts[:, pair[qk], qk, b, :]).then_inc(stacked[b], 16)
                if b == 0:
                    sp.dma_start(x_res[:], x_nat.rearrange("b (c p) n -> p (b c) n", p=P)).then_inc(ld["x"], 16)
                    sp.dma_start(bo[:], b_out.partition_broadcast(P)).then_inc(ld["bo"], 16)
                    sp.dma_start(wfc[:], w_fc.rearrange("(c p) n -> p c n", p=P)).then_inc(ld["wfc"], 16)
                    sp.dma_start(wpj[:], w_proj.rearrange("(c p) n -> p c n", p=P)).then_inc(ld["wpj"], 16)
                    sp.dma_start(wo[:], w_out.rearrange("(c p) n -> p c n", p=P)).then_inc(ld["wo"], 16)
            sp.dma_start(maskb[:], mask_in.rearrange("b a n -> (a b) n").partition_broadcast(P))\
                .then_inc(ld["mask"], 16)

            for b in range(2, B):
                sp.wait_ge(stacked[b], 12 * 16)
                sp.nop().then_inc(stack_ready, 1)

            out_v = out.rearrange("b (c p) n -> p (b c) n", p=P)
            for n in range(B - 1):
                sp.wait_ge(y_done, 2 * n + 2)
                sp.dma_start(out_v[:, 2 * n:2 * n + 2, :], y_out[:, 2 * n:2 * n + 2, :]).then_inc(stored, 16)
            for k in range(TB - 2, TB):
                sp.wait_ge(y_done, k + 1)
                sp.dma_start(out_v[:, k:k + 1, :], y_out[:, k:k + 1, :]).then_inc(stored, 16)
            sp.wait_ge(stored, 16 * (B + 1))

        @blk_ctx.gpsimd
        def _(pool):
            steps = [0]

            def step(ins):
                steps[0] += 1
                ins.then_inc(pool_step, 1)
                pool.wait_ge(pool_step, steps[0])

            nc.gpsimd.memset(negm_p[:], 0.0).then_inc(zeros, 1)
            nc.gpsimd.memset(ones_b[:], 1.0).then_inc(consts, 1)
            nc.gpsimd.memset(v_ones[:], 1.0).then_inc(consts, 1)
            nc.gpsimd.memset(expo[:], -0.5)
            nc.gpsimd.memset(mask_qk[:], 0.0)
            nc.gpsimd.memset(mask_kq[:], 0.0)
            step(nc.gpsimd.memset(ident_f[:], 0.0))
            nc.gpsimd.affine_select(out=mask_qk[:], in_=mask_qk[:], compare_op=ALU.is_ge, fill=MASKED,
                                    base=0, pattern=[[0, 2], [-1, P]], channel_multiplier=1)
            nc.gpsimd.affine_select(out=mask_kq[:], in_=mask_kq[:], compare_op=ALU.is_ge, fill=MASKED,
                                    base=0, pattern=[[0, 2], [1, P]], channel_multiplier=-1)
            step(nc.gpsimd.affine_select(out=ident_f[:], in_=ident_f[:], compare_op=ALU.not_equal, fill=1.0,
                                         base=0, pattern=[[-1, P]], channel_multiplier=1))
            nc.gpsimd.tensor_copy(ident[:], ident_f[:]).then_inc(consts, 1)
            for stack, row in ((stack_q, ROW_BIAS), (stack_k, ROW_MAX)):
                pool.dma_start(stack[row:row + 3, :].rearrange("p (a t) -> p a t", a=B * H // 4),
                               ones_b[:].unsqueeze(1).to_broadcast([3, B * H // 4, T])).then_inc(stack_const, 16)
            pool.dma_start(stack_k[ROW_BIAS:ROW_BIAS + 3, :].rearrange("p (b n) -> p b n", b=B),
                           alibi.unsqueeze(1).to_broadcast([3, B, H * S])).then_inc(stack_const, 16)

            def third_part(n):
                pool.wait_ge(qk_p1, n + 1)
                nc.gpsimd.tensor_tensor(out=unit_part(n, 2), in0=qk_r[:, n % 2, :].rearrange("p (b t) -> p b t", b=2),
                                        in1=unit_part(n, 1), op=ALU.subtract).then_inc(qk_p2, 1)

            for n in range(4):
                third_part(n)
            pool.wait_ge(ctx_max, 1)
            nc.gpsimd.partition_all_reduce(sc[:, 1:2], sc[:, 0:1], P, bass.bass_isa.ReduceOp.max)\
                .then_inc(ctx_all, 1)

            def rstds(n, of=(0, 1)):
                first, last = of[0], of[-1]
                wait_apart(pool, aggr_done, 2 * n + last + 1)
                later = isinstance(n, int) and n >= B
                side = n % 2 if later else 0
                if later and n >= B + 2 and first == 0:
                    u = n - 2 - B
                    pool.wait_ge(x2_done if u < B else y_done, 2 * (u % B) + 2)
                nc.gpsimd.tensor_scalar(ve[:, side, first:last + 1], mv[:, side, first:last + 1, 1], LN_EPS, None,
                                        ALU.add).then_inc(ve_done, 1)
                if later:
                    nc.gpsimd.tensor_scalar(nmean[:, side, first:last + 1], mv[:, side, first:last + 1, 0], -1.0,
                                            None, ALU.mult)
                before = n + (1 if len(of) == 1 and first == 1 else 0)
                pool.wait_ge(ve_done, before + 1)
                nc.gpsimd.tensor_tensor(out=rstd[:, side, first:last + 1], in0=ve[:, side, first:last + 1],
                                        in1=expo[:, first:last + 1], op=ALU.pow)\
                    .then_inc(pow_done if later else rstd_done, 1)
                if later:
                    pool.wait_ge(pow_done, before - B + 1)
                    nc.gpsimd.tensor_tensor(out=nbias[:, side, first:last + 1], in0=nmean[:, side, first:last + 1],
                                            in1=rstd[:, side, first:last + 1], op=ALU.mult).then_inc(rstd_done, 1)

            def add_mask(b):
                pool.wait_ge(x1_done, 2 * b + 2)
                nc.gpsimd.tensor_tensor(out=x1m[:, 2 * b:2 * b + 2, :], in0=x1[:, 2 * b:2 * b + 2, :],
                                        in1=maskb[:, b, :].unsqueeze(1).to_broadcast([P, 2, D]),
                                        op=ALU.add).then_inc(x1m_done, 1)

            for n in range(4, 8):
                third_part(n)
            pool.wait_ge(ld["x"], 16)
            pool.wait_ge(ld["bo"], 16)
            nc.gpsimd.tensor_tensor(out=x_res[:], in0=x_res[:],
                                    in1=bo[:].unsqueeze(1).to_broadcast([P, TB, D]),
                                    op=ALU.add).then_inc(xres_done, 1)
            pool.wait_ge(wsum, 2)
            step(nc.gpsimd.partition_all_reduce(sc[:, 4:6], sc[:, 2:4], P, bass.bass_isa.ReduceOp.add))
            step(nc.gpsimd.tensor_scalar(sc[:, 14:16], sc[:, 4:6], 1.0 / (D * F), 1e-5, ALU.mult, ALU.max))
            nc.gpsimd.tensor_scalar(sc[:, 16:18], sc[:, 14:16], 0.7, None, ALU.mult)
            nc.gpsimd.tensor_scalar(sc[:, 18:20], sc[:, 14:16], -0.7, None, ALU.mult)
            step(nc.gpsimd.tensor_tensor(out=sc[:, 22:23], in0=sc[:, 14:15], in1=sc[:, 14:15], op=ALU.mult))
            step(nc.gpsimd.tensor_tensor(out=sc[:, 23:24], in0=sc[:, 22:23], in1=sc[:, 15:16], op=ALU.mult))
            nc.gpsimd.tensor_scalar(sc[:, 24:25], sc[:, 23:24], H_SCALE ** -2, None, ALU.mult)\
                .then_inc(tern_done, 1)

            def round_context(n):
                pool.wait_ge(kv_magic, n + 1)
                k2, m2 = kv_ctx[:, 2 * n:2 * n + 2, :], magic[:, 2 * n:2 * n + 2, :]
                step(nc.gpsimd.tensor_tensor(out=k2, in0=k2, in1=m2, op=ALU.add))
                nc.gpsimd.tensor_tensor(out=kv_q[:, 2 * n:2 * n + 2, :], in0=k2, in1=m2, op=ALU.subtract)\
                    .then_inc(kvq_done, 1)

            def body(b, prev, nxt):
                if not prev:
                    round_context(0)
                    round_context(1)
                if not nxt:
                    round_context(2)
                    round_context(3)
                    pool.wait_ge(ld["mask"], 16)
                    add_mask(0)
                    add_mask(1)
                if prev:
                    rstds(b - 1)

            body(0, False, True)
            with pool.Fori(1, B - 1) as b:
                body(b, True, True)
            body(B - 1, True, False)
            add_mask(B - 2)
            rstds(B - 1)
            pool.wait_ge(x_max, 1)
            nc.gpsimd.partition_all_reduce(sc[:, 11:12], sc[:, 10:11], P, bass.bass_isa.ReduceOp.max)\
                .then_inc(x_all, 1)

            def scale_x1(n):
                pool.wait_ge(xs_done, 1)
                nc.gpsimd.tensor_scalar(xy[:, 2 * n:2 * n + 2, :], x1[:, 2 * n:2 * n + 2, :], sc[:, 12:13], FP8_MAX,
                                        ALU.mult, ALU.min).then_inc(x_scaled, 1)

            for n in range(1, B):
                scale_x1(n)
            rstds(B)
            add_mask(B - 1)
            for n in range(B + 1, 2 * B):
                rstds(n)

            def hidden_high(n):
                half, hc = divmod(n, FC)
                pool.wait_ge(hs_done, n + 1)
                nc.gpsimd.tensor_scalar(h_hi[:, hc, half * HALF:(half + 1) * HALF], hs[:, n % 2, :], 1.0, 0.0,
                                        ALU.mult, ALU.add).then_inc(hhi_done, 1)

            for n in range(2 * FC):
                hidden_high(n)
            for n in range(2 * B, 3 * B - 1):
                rstds(n)
            rstds(3 * B - 1, (0,))
            rstds(3 * B - 1, (1,))

        @blk_ctx.scalar
        def _(act):
            act.dma_start(bqk[:], b_qk).then_inc(ld["bqk"], 16)
            act.dma_start(wv[:], w_v.rearrange("(c p) n -> p c n", p=P)).then_inc(ld["wv"], 16)
            act.dma_start(bv[:], b_v.partition_broadcast(P)).then_inc(ld["bv"], 16)
            act.dma_start(kv_ctx[:], ctx_in.rearrange("b (c p) n -> p (b c) n", p=P)).then_inc(ld["ctx"], 16)

            act.wait_ge(zeros, 1)
            nc.scalar.activation(sc[:, 31:32], negm_p[:, 0, 0, 0, 0:1], ACT.Exp)
            act.wait_ge(bq_done, 1)

            def qk_first(n):
                half, j = units[n]
                act.wait_ge(qk_mm, n + 1)
                wait(act, qk_r1, n - 1)
                nc.scalar.activation(qk_t[:, n % 2, :], ps[:, 4 + n % 4, :], ACT.Identity, bias=bqk[:, j:j + 1],
                                     scale=HD ** -0.5 if j < 2 else 1.0).then_inc(qk_f32, 1)
                act.wait_ge(qk_f32, n + 1)
                nc.scalar.activation(unit_part(n, 0), qk_t[:, n % 2, :].rearrange("p (b t) -> p b t", b=2),
                                     ACT.Copy).then_inc(qk_p0, 1)

            def qk_second(n):
                act.wait_ge(qk_r1, n + 1)
                nc.scalar.activation(unit_part(n, 1), qk_r[:, n % 2, :].rearrange("p (b t) -> p b t", b=2),
                                     ACT.Copy).then_inc(qk_p1, 1)

            def send_max(b, half):
                act.wait_ge(mT_done, 2 * b + half + 1)
                act.dma_start(stack_q[ROW_MAX:ROW_MAX + 3, cols(b, HC * half, 0, HC * S)], negm_T[:, half, :])\
                    .then_inc(mrows, 16)

            def sum_weights(w, col):
                nc.scalar.activation(pT[:].rearrange("p a n -> p (a n)")[:, 0:FC * D],
                                     w[:].rearrange("p a n -> p (a n)"), ACT.Abs,
                                     accum_out=sc[:, col:col + 1]).then_inc(wsum, 1)

            for n in range(8):
                qk_first(n)
                if n % 4 > 0:
                    qk_second(n - 1)
                if n == 3:
                    qk_second(n)
            act.wait_ge(ctx_scaled, 1)
            for n in range(B):
                nc.scalar.activation(kv_ctx[:, 2 * n:2 * n + 2, :], kv_ctx[:, 2 * n:2 * n + 2, :], ACT.Copy,
                                     scale=sc[:, 8:9]).then_inc(kv_scaled, 1)
            qk_second(7)
            send_max(0, 0)
            act.wait_ge(ld["wfc"], 16)
            sum_weights(wfc, 2)
            act.wait_ge(ld["wpj"], 16)
            act.wait_ge(wsum, 1)
            sum_weights(wpj, 3)

            def exps(b, p):
                for i in (2 * p, 2 * p + 1):
                    act.wait_ge(st_mm, b * H + i + 1)
                    if i % 4 == 0:
                        wait(act, pv_mm, b * GROUPS + i // 4 - 1)
                    nc.scalar.activation(pT[:, i % P_SLOTS, :], ps[:, BANK_ST + i % 2, 0:TRI], ACT.Exp)\
                        .then_inc(exp_done, 1)

            def copy_o(b, i):
                act.wait_ge(pv_mm, b * GROUPS + 2 * i + 2)
                wait(act, ot_mm, b * 2)
                nc.scalar.activation(o_raw[:, 2 * i:2 * i + 2, :].rearrange("p g q -> p (g q)"),
                                     ps[:, BANK_O, :], ACT.Copy).then_inc(o_copied, 1)

            def copy_oT(b):
                act.wait_ge(oT_mm, b + 1)
                wait(act, y_mm, b)
                nc.scalar.activation(oT[:].rearrange("p c q -> p (c q)"), ps[:, BANK_Y, :], ACT.Copy)\
                    .then_inc(oT_done, 1)

            def copy_values(b):
                wait(act, pv_mm, b * GROUPS)
                nc.scalar.activation(v_ones[:, :, :, 0:HD],
                                     v_nat[:, blocks(b), :].rearrange("p k (h d) -> p k h d", h=H), ACT.Copy)\
                    .then_inc(vb_done, 1)

            def body(b, prev, nxt):
                for p in range(PAIRS):
                    exps(b, p)
                    if p == 0 and prev:
                        copy_o(b - 1, 1)
                    if p == 2:
                        send_max(b, 1)
                        copy_values(b)
                    if p == 4 and prev:
                        copy_oT(b - 1)
                    if p == 5:
                        copy_o(b, 0)
                        if nxt:
                            send_max(b + 1, 0)

            act.wait_ge(v_done, 4)
            act.wait_ge(consts, 2)
            act.wait_ge(wsum, 2)
            body(0, False, True)
            with act.Fori(1, B - 1) as b:
                body(b, True, True)
            body(B - 1, True, False)
            copy_o(B - 1, 1)
            act.wait_ge(y_mm, B - 1)
            for i in range(2):
                act.wait_ge(oT_mm, B + i)
                nc.scalar.activation(oT[:, :, i * P:(i + 1) * P],
                                     ps[:, BANK_SM + 2 + i, 0:D].rearrange("p (c q) -> p c q", c=DC), ACT.Copy)\
                    .then_inc(oT_done, 1)

            def turned(n):
                act.wait_ge(xqT_mm, n + 1)
                nc.scalar.activation(x_qT[:, :, n * S:(n + 1) * S],
                                     ps[:, n % 2, 0:S].bitcast(BF16).rearrange("p (c t) -> p c t", c=DC),
                                     ACT.Copy).then_inc(xqT_done, 1)

            def norm(dst, n, u, signal):
                for i in range(2):
                    k = 2 * n + i
                    act.wait_ge(rstd_done, u + 1 + (i if u == 3 * B - 1 else 0))
                    nc.scalar.activation(dst[:, k, :], r1[:, k, :], ACT.Identity, bias=nbias[:, u % 2, i:i + 1],
                                         scale=rstd[:, u % 2, i:i + 1]).then_inc(signal, 1)

            def x2_high(n):
                act.wait_ge(x2T_mm, n + 1)
                nc.scalar.activation(x2_hi[:, :, n * S:(n + 1) * S],
                                     ps[:, 4 + n % 2, :].rearrange("p (c t) -> p c t", c=DC), ACT.Copy)\
                    .then_inc(x2hi_done, 1)

            def hidden(n):
                act.wait_ge(f1_mm, n + 1)
                nc.scalar.activation(hu[:, n % 2, :], ps[:, F1_BANKS[n % 4], :], ACT.Relu, scale=H_SCALE)\
                    .then_inc(hu_done, 1)
                act.wait_ge(hu_done, n + 1)
                wait(act, hlo_done, n - 1)
                nc.scalar.activation(hs[:, n % 2, :], hu[:, n % 2, :], ACT.Square).then_inc(hs_done, 1)

            for n in range(B + 2):
                if n >= 2:
                    norm(x2, n - 2, B + n - 2, x2_done)
                    if n == B + 1:
                        hidden(1)
                    x2_high(n - 2)
                if n < B:
                    turned(n)
                if n == B:
                    hidden(0)
            for n in range(2, 2 * FC):
                hidden(n)
            for n in range(B):
                norm(y_out, n, 2 * B + n, y_done)

        @blk_ctx.vector
        def _(dve):
            v = nc.vector
            steps = [0]

            def step(ins):
                steps[0] += 1
                ins.then_inc(dve_step, 1)
                dve.wait_ge(dve_step, steps[0])

            dve.wait_ge(ld["bqk"], 16)
            v.tensor_scalar(bqk[:, 0:2], bqk[:, 0:2], HD ** -0.5, None, ALU.mult).then_inc(bq_done, 1)

            def qk_parts(n):
                wait(dve, qk_p2, n - 1)
                t3, r3 = (a[:, n % 2, :].rearrange("p (b t) -> p b t", b=2) for a in (qk_t, qk_r))
                dve.wait_ge(qk_p0, n + 1)
                v.tensor_tensor(out=r3, in0=t3, in1=unit_part(n, 0), op=ALU.subtract).then_inc(qk_r1, 1)

            def values_out(n):
                dve.wait_ge(v_mm, n + 1)
                if n == 0:
                    dve.wait_ge(ld["bv"], 16)
                v.tensor_tensor(out=v_nat[:, 2 * n:2 * n + 2, :],
                                in0=ps[:, n, :].rearrange("p (k n) -> p k n", k=2),
                                in1=bv[:].unsqueeze(1).to_broadcast([P, 2, D]), op=ALU.add)\
                    .then_inc(v_done, 1)

            def fp8_scale(amax, scale, inverse, done):
                step(v.tensor_scalar(sc[:, 20:21], amax, FP8_EPS, None, ALU.max))
                step(v.reciprocal(sc[:, 21:22], sc[:, 20:21]))
                v.tensor_scalar(scale, sc[:, 21:22], FP8_MAX, None, ALU.mult).then_inc(done, 1)
                v.tensor_scalar(inverse, sc[:, 20:21], 1.0 / FP8_MAX, None, ALU.mult).then_inc(done, 1)

            def rounding(dst, y):
                step(v.tensor_scalar(dst.bitcast(I32), y.bitcast(I32), EXPONENT, None, ALU.bitwise_and))
                return v.tensor_scalar(dst, dst, FP8_SMALLEST, 1.5 * 2.0 ** 20, ALU.max, ALU.mult)

            for n in range(4):
                qk_parts(n)
            dve.wait_ge(ld["ctx"], 16)
            v.tensor_reduce(sc[:, 0:1], kv_ctx[:].rearrange("p a n -> p (a n)"), AX.X, ALU.max,
                            apply_absolute_value=True).then_inc(ctx_max, 1)
            for n in range(TB // 2):
                values_out(n)
            dve.wait_ge(ctx_all, 1)
            fp8_scale(sc[:, 1:2], sc[:, 8:9], sc[:, 9:10], ctx_scaled)

            def row_max(b, p):
                dve.wait_ge(smax_mm, b * PAIRS + p + 1)
                if p in (1, 4):
                    wait(dve, mT_mm, 2 * b + p // 4)
                if p % 4 == 0:
                    wait(dve, mparts, 6 * (2 * b + p // 4))
                bank = BANK_SM + 2 * (p % 2)
                v.tensor_reduce(negm3[:, 2 * p:2 * p + 2, :],
                                ps[:, bank:bank + 2, 0:TRI].rearrange("p e (a k) -> p e a k", k=P), AX.X, ALU.max,
                                negate=True).then_inc(smax_red, 1)

            def max_parts(b, half):
                done = 6 * (2 * b + half)
                dve.wait_ge(smax_red, b * PAIRS + 4 * half + 4)
                wait(dve, mT_mm, 2 * b + half - 1)
                if isinstance(b, int) and b == 0 and half == 0:
                    dve.wait_ge(zeros, 1)
                three = negm3[:, HC * half:HC * (half + 1), :]
                negm, (r0, r1_), (p0, p1, p2) = (three[:, :, 0:2].rearrange("p h k -> p k h"),
                                                 (negm_r[:, 0], negm_r[:, 1]),
                                                 (negm_p[:, half, :, part, :] for part in range(3)))
                v.tensor_tensor(out=three[:, :, 1], in0=three[:, :, 1], in1=three[:, :, 2], op=ALU.min)\
                    .then_inc(mparts, 1)
                dve.wait_ge(mparts, done + 1)
                v.tensor_copy(p0, negm).then_inc(mparts, 1)
                dve.wait_ge(mparts, done + 2)
                v.tensor_tensor(out=r0, in0=negm, in1=p0, op=ALU.subtract).then_inc(mparts, 1)
                dve.wait_ge(mparts, done + 3)
                v.tensor_copy(p1, r0).then_inc(mparts, 1)
                dve.wait_ge(mparts, done + 4)
                v.tensor_tensor(out=r1_, in0=r0, in1=p1, op=ALU.subtract).then_inc(mparts, 1)
                dve.wait_ge(mparts, done + 5)
                v.tensor_copy(p2, r1_).then_inc(mparts, 1)

            def copy_max(b, half):
                dve.wait_ge(mT_mm, 2 * b + half + 1)
                wait(dve, mrows, 16 * (2 * b + half - 1))
                v.tensor_copy(negm_T[:, half, :], ps[0:3 * HC, MT_BANK[half], TRI:512].bitcast(BF16))\
                    .then_inc(mT_done, 1)

            def normalise(b, i, bank):
                dve.wait_ge(ot_mm, 2 * b + i + 1)
                wait(dve, oT_mm, b)
                heads = ps[:, bank, :].rearrange("p (h d) -> p h d", d=2 * HD)
                v.reciprocal(rden[:, i, :].unsqueeze(2), heads[:, :, HD:HD + 1]).then_inc(rden_done, 1)
                dve.wait_ge(rden_done, 2 * b + i + 1)
                for c in range(DC):
                    last = v.tensor_tensor(out=o_nrm[:, i, c * P:(c + 1) * P].rearrange("p (h d) -> p h d", d=HD),
                                           in0=heads[:, c:H:DC, 0:HD],
                                           in1=rden[:, i, c:H:DC].unsqueeze(2).to_broadcast([P, HC, HD]),
                                           op=ALU.mult)
                last.then_inc(o_done, 1)

            def add_residual(b):
                dve.wait_ge(y_mm, b + 1)
                v.tensor_tensor(out=r1[:, blocks(b), :], in0=ps[:, BANK_Y, :].rearrange("p (k n) -> p k n", k=2),
                                in1=x_res[:, blocks(b), :], op=ALU.add).then_inc(r1_done, 1)
                statistics(lambda i: r1[:, block(b, i), :], b, 0, r1_done, b + 1)

            def sums_of_block(rows, n, i):
                if i == 0:
                    wait(dve, aggr_done, 2 * n)
                v.bn_stats(stats[:, i, :], rows(i)).then_inc(stat_done, 1)

            def aggregate(n, parity, of=(0, 1)):
                if isinstance(n, int) and n >= B:
                    dve.wait_ge(rstd_done, n - 1)
                for i in of:
                    wait_apart(dve, stat_done, 2 * n + i + 1)
                    v.bn_aggr(mv[:, parity, i, :], stats[:, i, :]).then_inc(aggr_done, 1)

            def statistics(rows, n, parity, summed, count):
                wait_apart(dve, summed, count)
                for i in range(2):
                    sums_of_block(rows, n, i)
                aggregate(n, parity)

            def first_norm(b):
                dve.wait_ge(rstd_done, b + 1)
                for i in range(2):
                    v.tensor_scalar(x1[:, block(b, i), :], r1[:, block(b, i), :], mv[:, 0, i, 0:1],
                                    rstd[:, 0, i:i + 1], ALU.subtract, ALU.mult).then_inc(x1_done, 1)
                dve.wait_ge(x1_done, 2 * b + 2)
                v.tensor_reduce(amax[:, b:b + 1] if isinstance(b, int) else amax[:, bass.ds(b, 1)],
                                x1[:, blocks(b), :], AX.XY, ALU.max, apply_absolute_value=True).then_inc(b_max, 1)

            def ternarise(i):
                w2, wt2 = ((wfc, wfc_t), (wpj, wpj_t))[i]
                w2, wt2 = w2[:].rearrange("p a n -> p (a n)"), wt2[:].rearrange("p a n -> p (a n)")
                dve.wait_ge(tern_done, 1 + i)
                step(v.tensor_scalar(w_low[:], w2, sc[:, 18 + i:19 + i], None, ALU.is_lt))
                v.scalar_tensor_tensor(wt2, w2, sc[:, 16 + i:17 + i], w_low[:], ALU.is_gt, ALU.subtract)\
                    .then_inc(tern_done, 1)

            def context_magic(n):
                dve.wait_ge(kv_scaled, n + 1)
                k2 = kv_ctx[:, 2 * n:2 * n + 2, :]
                step(v.tensor_scalar(k2, k2, FP8_MAX, -FP8_MAX, ALU.min, ALU.max))
                rounding(magic[:, 2 * n:2 * n + 2, :], kv_ctx[:, 2 * n:2 * n + 2, :]).then_inc(kv_magic, 1)

            def body(b, prev, nxt):
                for p in range(PAIRS):
                    if prev and p == 2:
                        normalise(b - 1, 0, BANK_Y)
                        normalise(b - 1, 1, BANK_O)
                    if nxt:
                        row_max(b + 1, p)
                    if p == 1:
                        copy_max(b, 1)
                    if nxt and p == 3:
                        max_parts(b + 1, 0)
                    if nxt and p == 4:
                        copy_max(b + 1, 0)
                    if nxt and p == 7:
                        max_parts(b + 1, 1)
                    if prev and p == 5:
                        add_residual(b - 1)
                    if prev and p == 7:
                        first_norm(b - 1)
                    if not prev and p in (4, 6):
                        context_magic(p // 2 - 2)
                    if not nxt and p in MAGIC_PAIRS:
                        context_magic(2 + MAGIC_PAIRS.index(p))
                    if not nxt and p == 5:
                        ternarise(0)

            for p in range(PAIRS):
                row_max(0, p)
                if p == 3:
                    max_parts(0, 0)
                if p == 4:
                    copy_max(0, 0)
                if p < 3 or p == 4:
                    qk_parts(4 + min(p, 3))
            max_parts(0, 1)
            body(0, False, True)
            dve.wait_ge(xres_done, 1)
            with dve.Fori(1, B - 1) as b:
                body(b, True, True)
            body(B - 1, True, False)
            normalise(B - 1, 0, BANK_SM)
            normalise(B - 1, 1, BANK_SM + 1)
            for i in range(2):
                k = 2 * (B - 1) + i
                dve.wait_ge(y_mm, B + i)
                v.tensor_tensor(out=r1[:, k, :], in0=ps[:, BANK_ST + i, 0:D], in1=x_res[:, k, :], op=ALU.add)\
                    .then_inc(r1_done, 1)
                dve.wait_ge(r1_done, B + i)
                sums_of_block(lambda i: r1[:, 2 * (B - 1) + i, :], B - 1, i)
            aggregate(B - 1, 0)
            first_norm(B - 1)

            dve.wait_ge(b_max, B)
            v.tensor_reduce(sc[:, 10:11], amax[:], AX.X, ALU.max).then_inc(x_max, 1)
            dve.wait_ge(x_all, 1)
            fp8_scale(sc[:, 11:12], sc[:, 12:13], sc[:, 13:14], xs_done)
            dve.wait_ge(xs_done, 1)

            def unit(a, n):
                return a[:, 2 * n:2 * n + 2, :].rearrange("p a n -> p (a n)")

            def quantise(n, k):
                x, y, m = unit(x1, n), unit(xy, n), qe[:, n % 2, :]
                if k == 0 and n > 0:
                    return
                if k == 1 and n > 0:
                    dve.wait_ge(x_scaled, n)
                elif k > 0:
                    dve.wait_ge(q_step, 3 * n + k)
                if k == 0:
                    v.tensor_scalar(y, x, sc[:, 12:13], FP8_MAX, ALU.mult, ALU.min).then_inc(q_step, 1)
                elif k == 1:
                    wait(dve, xq_done, n - 1)
                    v.tensor_scalar(m.bitcast(I32), y.bitcast(I32), EXPONENT, None, ALU.bitwise_and)\
                        .then_inc(q_step, 1)
                elif k == 2:
                    v.tensor_scalar(m, m, FP8_SMALLEST, 1.5 * 2.0 ** 20, ALU.max, ALU.mult).then_inc(q_step, 1)
                elif k == 3:
                    v.scalar_tensor_tensor(y, y, -FP8_MAX, m, ALU.max, ALU.add).then_inc(q_step, 1)
                else:
                    v.tensor_tensor(out=unit(x_q, n), in0=y, in1=m, op=ALU.subtract).then_inc(xq_done, 1)

            def cross_residual(n, k):
                if k == 0:
                    dve.wait_ge(xa_mm, n + 1)
                    dve.wait_ge(x1m_done, n + 1)
                    v.scalar_tensor_tensor(unit(r1, n), ps[:, 2 + n % 2, :], sc[:, 25:26], unit(x1m, n),
                                           ALU.mult, ALU.add).then_inc(r2_done, 1)
                elif k == 1:
                    dve.wait_ge(r2_done, n + 1)
                    sums_of_block(lambda i: r1[:, 2 * n + i, :], B + n, 0)
                elif k == 2:
                    sums_of_block(lambda i: r1[:, 2 * n + i, :], B + n, 1)
                else:
                    aggregate(B + n, (B + n) % 2)

            def x2_low(n):
                dve.wait_ge(x2hi_done, n + 1)
                v.tensor_tensor(out=x2_lo[:, :, n * S:(n + 1) * S],
                                in0=ps[:, 4 + n % 2, :].rearrange("p (c t) -> p c t", c=DC),
                                in1=x2_hi[:, :, n * S:(n + 1) * S], op=ALU.subtract).then_inc(x2lo_done, 1)

            def hidden(n):
                half, hc = divmod(n, FC)
                dve.wait_ge(hhi_done, n + 1)
                v.tensor_tensor(out=h_lo[:, hc, half * HALF:(half + 1) * HALF], in0=hs[:, n % 2, :],
                                in1=h_hi[:, hc, half * HALF:(half + 1) * HALF], op=ALU.subtract)\
                    .then_inc(hlo_done, 1)

            def last_residual(n):
                dve.wait_ge(f2_mm, n + 1)
                v.scalar_tensor_tensor(unit(r1, n), ps[:, 2 + n, :], sc[:, 24:25], unit(x2, n),
                                       ALU.mult, ALU.add).then_inc(r3_done, 1)
                statistics(lambda i: r1[:, 2 * n + i, :], 2 * B + n, (2 * B + n) % 2, r3_done, n + 1)

            for n in range(B + 2):
                for k in range(5):
                    if n < B:
                        quantise(n, k)
                    if 1 <= n < B + 1 and k == 3:
                        cross_residual(n - 1, 0)
                if 1 <= n < B + 1:
                    for k in range(1, 4):
                        cross_residual(n - 1, k)
                if n == 0:
                    dve.wait_ge(xs_done, 2)
                    step(v.tensor_tensor(out=sc[:, 25:26], in0=sc[:, 13:14], in1=sc[:, 9:10], op=ALU.mult))
                if n == B + 1:
                    hidden(0)
                if n >= 2:
                    x2_low(n - 2)
                if n == B:
                    ternarise(1)
            for n in range(1, 2 * FC):
                hidden(n)
                if n == 2 * FC - RESIDUAL_AT:
                    last_residual(0)
            for n in range(1, B - 1):
                last_residual(n)
            n = B - 1
            for i in range(2):
                dve.wait_ge(f2_mm, B + i)
                v.scalar_tensor_tensor(r1[:, 2 * n + i, :], ps[:, LAST_BANKS[i], i * D:(i + 1) * D], sc[:, 24:25],
                                       x2[:, 2 * n + i, :], ALU.mult, ALU.add).then_inc(r3_done, 1)
                dve.wait_ge(r3_done, B + i)
                sums_of_block(lambda i: r1[:, 2 * n + i, :], 3 * B - 1, i)
                aggregate(3 * B - 1, (3 * B - 1) % 2, (i,))

        @blk_ctx.tensor
        def _(pe):
            mm = nc.tensor.matmul
            pe.wait_ge(zeros, 1)
            idle = negm_p[:, 0].rearrange("p i a h -> p (i a h)")
            for n in range(WARM_START):
                mm(ps[:, n % 4, 0:2 * P], idle[:, 0:P], idle, start=True, stop=True)

            def keep_warm(count, bank):
                for n in range(count):
                    mm(ps[:, bank, 0:2 * P], ident[:], mask_qk[:], start=True, stop=True)

            def project_qk(n):
                half, j = units[n]
                if j == 0:
                    pe.wait_ge(ld[f"xT{half}"], 16)
                if n == 1:
                    pe.wait_ge(ld["wqk"], 16)
                wait(pe, qk_f32, n - 3)
                for c in range(DC):
                    last = mm(ps[:, 4 + n % 4, :], wqk[:, c, j, :], xT[:, c, half * HALF:(half + 1) * HALF],
                              start=(c == 0), stop=(c == DC - 1))
                last.then_inc(qk_mm, 1)

            pe.wait_ge(ld["wq0"], 16)
            for n in range(4):
                project_qk(n)
            pe.wait_ge(ld["wv"], 16)
            pe.wait_ge(ld["xT1"], 16)
            for n in range(TB // 2):
                for i in range(2):
                    k = 2 * n + i
                    for c in range(DC):
                        last = mm(ps[:, n, i * D:(i + 1) * D], xT[:, c, k * P:(k + 1) * P], wv[:, c, :],
                                  start=(c == 0), stop=(c == DC - 1))
                last.then_inc(v_mm, 1)

            def score_max(b, p):
                wait(pe, smax_red, b * PAIRS + p - 1)
                if p == 6:
                    pe.wait_ge(mT_done, 2 * b + 1)
                if p == 3:
                    wait(pe, mT_done, 2 * b)
                for e in range(2):
                    i, bank = 2 * p + e, BANK_SM + 2 * (p % 2) + e
                    mm(diag(bank), ident[:], mask_qk[:], start=True, stop=False, skip_group_check=True)
                    mm(ps[:, bank, 0:P], stack_q[0:ROW_MAX, cols(b, i, 0, P)], stack_k[0:ROW_MAX, cols(b, i, 0, P)],
                       start=False, stop=False, skip_group_check=True)
                    last = mm(ps[:, bank, P:TRI], stack_q[0:ROW_MAX, cols(b, i, P, P)],
                              stack_k[0:ROW_MAX, cols(b, i, 0, S)], start=False, stop=True, skip_group_check=True)
                last.then_inc(smax_mm, 1)

            def scores(b, p):
                if p % 4 == 0:
                    pe.wait_ge(mrows, 16 * (2 * b + p // 4 + 1))
                for i in (2 * p, 2 * p + 1):
                    wait(pe, exp_done, b * H + i - 1)
                    bank = BANK_ST + i % 2
                    mm(diag(bank), ident[:], mask_kq[:], start=True, stop=False, skip_group_check=True)
                    mm(ps[:, bank, 0:S], stack_k[0:ROWS, cols(b, i, 0, P)], stack_q[0:ROWS, cols(b, i, 0, S)],
                       start=False, stop=False, skip_group_check=True)
                    mm(ps[:, bank, S:TRI], stack_k[0:ROWS, cols(b, i, P, P)], stack_q[0:ROWS, cols(b, i, P, P)],
                       start=False, stop=True, skip_group_check=True).then_inc(st_mm, 1)

            def max_to_rows(b, half):
                pe.wait_ge(mparts, 6 * (2 * b + half + 1))
                spare = ps[:, MT_BANK[half], TRI:512]
                for i in range(2):
                    last = nc.tensor.transpose(spare[:, i * P // 2:(i + 1) * P // 2].bitcast(BF16),
                                               negm_p[:, half, i, :, :].rearrange("p a h -> p (a h)"), ident[:])
                last.then_inc(mT_mm, 1)

            def values(b, g):
                pe.wait_ge(exp_done, b * H + 4 * g + 4)
                if g == 0:
                    pe.wait_ge(vb_done, b + 1)
                    wait(pe, o_done, 2 * b)
                if g == 2:
                    pe.wait_ge(o_copied, 2 * b + 1)
                o = (g % 2) * S
                for k in range(2):
                    for j in range(4):
                        prob = pT[:, (4 * g + j) % P_SLOTS, :]
                        last = mm(ps[32 * j:32 * j + 32, BANK_O, o + k * P:o + S],
                                  v_ones[:, k, head(4 * g + j), :],
                                  prob[:, 0:S] if k == 0 else prob[:, S:TRI], start=(k == 0), stop=(k == 1),
                                  skip_group_check=True)
                last.then_inc(pv_mm, 1)

            def queries_down(b, i, bank):
                if i == 0:
                    pe.wait_ge(o_copied, 2 * b + 2)
                if isinstance(b, int) and b == B - 1 and i == 0:
                    pe.wait_ge(mT_done, 2 * B)
                for g in range(GROUPS):
                    last = nc.tensor.transpose(ps[:, bank, g * P:(g + 1) * P],
                                               o_raw[:, g, i * P:(i + 1) * P], ident_f[:])
                last.then_inc(ot_mm, 1)

            def features_down(b):
                pe.wait_ge(o_done, 2 * b + 2)
                for i in range(2):
                    for c in range(DC):
                        last = nc.tensor.transpose(ps[:, BANK_Y, c * S + i * P:c * S + (i + 1) * P],
                                                   o_nrm[:, i, c * P:(c + 1) * P], ident_f[:])
                last.then_inc(oT_mm, 1)

            def project(b):
                pe.wait_ge(oT_done, b + 1)
                for i in range(2):
                    for c in range(DC):
                        last = mm(ps[:, BANK_Y, i * D:(i + 1) * D], oT[:, c, i * P:(i + 1) * P], wo[:, c, :],
                                  start=(c == 0), stop=(c == DC - 1))
                last.then_inc(y_mm, 1)

            def body(b, prev, nxt):
                for p in range(PAIRS):
                    scores(b, p)
                    if p == 0 and prev and nxt:
                        pe.wait_ge(stack_ready, b)
                    if p == 5 and prev:
                        project(b - 1)
                    if nxt:
                        score_max(b + 1, p)
                    if p == 1:
                        max_to_rows(b, 1)
                    if p in (3, 5, 7):
                        values(b, (p - 3) // 2)
                    if p == 4 and nxt:
                        max_to_rows(b + 1, 0)
                    if p == 0 and prev:
                        values(b - 1, 3)
                    if p == 1 and prev:
                        queries_down(b - 1, 0, BANK_Y)
                        queries_down(b - 1, 1, BANK_O)
                    if p == 3 and prev:
                        features_down(b - 1)

            project_qk(4)
            pe.wait_ge(consts, 3)
            pe.wait_ge(stacked[0], 12 * 16)
            pe.wait_ge(stack_const, 3 * 16)
            pe.wait_ge(v_done, 4)
            for p in range(PAIRS):
                score_max(0, p)
                if p in (1, 2, 3):
                    project_qk(4 + p)
                if p == 4:
                    max_to_rows(0, 0)
                    pe.wait_ge(qk_f32, 8)
                if p >= 4:
                    keep_warm(WARM_MAXIMA, BANK_Y)
            pe.wait_ge(stacked[1], 12 * 16)
            pe.wait_ge(ld["wo"], 16)
            body(0, False, True)
            with pe.Fori(1, B - 1) as b:
                body(b, True, True)
            body(B - 1, True, False)
            values(B - 1, 3)
            queries_down(B - 1, 0, BANK_SM)
            queries_down(B - 1, 1, BANK_SM + 1)
            for i in range(2):
                pe.wait_ge(o_done, 2 * (B - 1) + i + 1)
                for c in range(DC):
                    last = nc.tensor.transpose(ps[:, BANK_SM + 2 + i, c * P:(c + 1) * P],
                                               o_nrm[:, i, c * P:(c + 1) * P], ident_f[:])
                last.then_inc(oT_mm, 1)
            for i in range(2):
                pe.wait_ge(oT_done, B + i)
                for c in range(DC):
                    last = mm(ps[:, BANK_ST + i, 0:D], oT[:, c, i * P:(i + 1) * P], wo[:, c, :],
                              start=(c == 0), stop=(c == DC - 1))
                last.then_inc(y_mm, 1)

            pe.wait_ge(kvq_done, 4)
            pe.wait_ge(r1_done, B + 1)

            def turn_values(n):
                pe.wait_ge(xq_done, n + 1)
                wait(pe, xqT_done, n - 1)
                tr = ps[:, n % 2, 0:S].bitcast(BF16)
                for i in range(2):
                    for c in range(DC):
                        last = nc.tensor.transpose(tr[:, c * S + i * P:c * S + (i + 1) * P],
                                                   x_q[:, 2 * n + i, c * P:(c + 1) * P], ident[:])
                last.then_inc(xqT_mm, 1)

            def cross(n):
                pe.wait_ge(xqT_done, n + 1)
                wait(pe, r2_done, n - 1)
                for i in range(2):
                    k = 2 * n + i
                    for c in range(DC):
                        last = mm(ps[:, 2 + n % 2, i * D:(i + 1) * D], x_qT[:, c, k * P:(k + 1) * P],
                                  kv_q[:, 2 * n + c, :], start=(c == 0), stop=(c == DC - 1))
                last.then_inc(xa_mm, 1)

            def turn_x2(n):
                pe.wait_ge(x2_done, 2 * n + 2)
                wait(pe, x2lo_done, n - 1)
                for i in range(2):
                    for c in range(DC):
                        last = nc.tensor.transpose(ps[:, 4 + n % 2, c * S + i * P:c * S + (i + 1) * P],
                                                   x2[:, 2 * n + i, c * P:(c + 1) * P], ident_f[:])
                last.then_inc(x2T_mm, 1)

            def hidden(n):
                half, hc = divmod(n, FC)
                if hc == 0:
                    pe.wait_ge(x2lo_done, 2 * half + 2)
                wait(pe, hu_done, n - 3)
                for c in range(DC):
                    for part in (x2_hi, x2_lo):
                        last = mm(ps[:, F1_BANKS[n % 4], :], wfc_t[:, c, hc * P:(hc + 1) * P],
                                  part[:, c, half * HALF:(half + 1) * HALF],
                                  start=(c == 0 and part is x2_hi), stop=(c == DC - 1 and part is x2_lo))
                last.then_inc(f1_mm, 1)

            def back(n):
                pe.wait_ge(tern_done, 3)
                pe.wait_ge(hlo_done, FC * (n // 2 + 1))
                for i in range(2):
                    k, bank = 2 * n + i, LAST_BANKS[i] if n == B - 1 else 2 + n
                    for hc in range(FC):
                        for part in (h_hi, h_lo):
                            last = mm(ps[:, bank, i * D:(i + 1) * D], part[:, hc, k * P:(k + 1) * P],
                                      wpj_t[:, hc, :], start=(hc == 0 and part is h_hi),
                                      stop=(hc == FC - 1 and part is h_lo))
                    if i == 1 or n == B - 1:
                        last.then_inc(f2_mm, 1)

            keep_warm(WARM_SCALE, F1_BANKS[0])
            for n in range(B + 2):
                if n >= 2:
                    turn_x2(n - 2)
                if n < B:
                    turn_values(n)
                    keep_warm(WARM_TURNED, F1_BANKS[0])
                    cross(n)
                    keep_warm(WARM_UNIT, F1_BANKS[0])
                if n == B:
                    pe.wait_ge(tern_done, 2)
                    for m in range(EARLY):
                        hidden(m)
            pe.wait_ge(r2_done, 4)
            for n in range(EARLY, 2 * FC):
                hidden(n)
            for n in range(B):
                back(n)


def kernel(x, ctx_2048, mask_Bx1xS2_ff0, L0_attn_Wqkv, L0_attn_b_qkv, L0_attn_Wout, L0_attn_b_out,
           L0_ffn_w_fc, L0_ffn_w_proj):
    import numpy as _np
    import concourse.bacc as _bacc
    from concourse import mybir as _mybir
    from concourse.bass_utils import run_bass_kernel_spmd as _run

    x, ctx, mask, wqkv, bqkv, wout, bout, wfc, wproj = (_np.asarray(a) for a in (
        x, ctx_2048, mask_Bx1xS2_ff0, L0_attn_Wqkv, L0_attn_b_qkv, L0_attn_Wout, L0_attn_b_out,
        L0_ffn_w_fc, L0_ffn_w_proj))
    w_qk = wqkv[:2 * D].reshape(4, HC, HD, D).transpose(3, 0, 2, 1).reshape(D, 4 * P)
    b_qk = bqkv[:2 * D].reshape(4, HC, HD).transpose(2, 1, 0).reshape(P, 4)
    slopes = 1.0 / 2.0 ** (_np.arange(1, H + 1, dtype=_np.float32) * _np.float32(8.0 / H))
    alibi = _np.arange(1 - S, 1, dtype=_np.float32)[None, :] * slopes.astype(_np.float32)[:, None]
    alibi = alibi.reshape(DC, HC, S).transpose(1, 0, 2).reshape(H * S)
    alibi_parts = _np.zeros((3, H * S), dtype=_mybir.dt.np(BF16))
    for part in range(3):
        alibi_parts[part] = alibi
        alibi = alibi - alibi_parts[part].astype(_np.float32)
    arrays = {
        "x_nat": x, "x_tr": x.reshape(T, D).T, "ctx_in": ctx, "mask_in": mask, "w_qk": w_qk, "b_qk": b_qk,
        "w_v": wqkv[2 * D:].T, "b_v": bqkv[2 * D:], "w_out": wout.T, "b_out": bout,
        "w_fc": wfc.T, "w_proj": wproj.T, "alibi": alibi_parts,
    }
    arrays = {n: _np.ascontiguousarray(a) for n, a in arrays.items()}
    nc = _bacc.Bacc("TRN2", target_bir_lowering=False, num_devices=1)
    args = [nc.dram_tensor(n, a.shape, _mybir.dt.from_np(a.dtype), kind="ExternalInput").ap()
            for n, a in arrays.items()]
    y = nc.dram_tensor("y", (B, S, D), F32, kind="ExternalOutput").ap()
    decoder_kernel(nc, *args, y)
    r = _run(nc, [arrays], core_ids=[0])
    return r.results[0]["y"]
```
